# Optimizing a Trainium2 kernel written in Bass

```python
import numpy as np
import jax
import jax.numpy as jnp

def _softmax(x, axis=-1):
    return jax.nn.softmax(x, axis=axis)

def _gelu(x):
    return jax.nn.gelu(x, approximate=True)

def _silu(x):
    return jax.nn.silu(x)

def _sigmoid(x):
    return jax.nn.sigmoid(x)

def _layernorm(x, axis=-1, eps=1e-05):
    m = jnp.mean(x, axis=axis, keepdims=True)
    v = jnp.var(x, axis=axis, keepdims=True)
    return (x - m) / jnp.sqrt(v + eps)

def _scatter_add(tgt, idx, src, axis=0):
    return tgt.at[idx].add(src)

def _segment_sum(src, seg, n):
    return jax.ops.segment_sum(src, seg, n)
kernel_name = 'mk_adj_ffn_d1_adj_r2_70ffa4'

def setup_inputs(seed: int=0):
    np.random.seed(seed)
    _w = jnp.asarray

    def _rec_inputs():
        import jax
        import jax.numpy as jnp
        _gk = jax.random.key(seed)
        x = -0.0002928 + 1 * jax.random.normal(jax.random.fold_in(_gk, 1), (128, 128, 128), jnp.float32)
        _a = jax.random.bernoulli(jax.random.fold_in(_gk, 2), 0.125, (128, 128, 128))
        _a = jnp.logical_or(_a, jnp.swapaxes(_a, -1, -2))
        _a = jnp.logical_or(_a, jnp.eye(128, dtype=bool))
        _af = _a.astype(jnp.float32)
        adj = _af
        return (x, adj)
    x, adj = _rec_inputs()

    def _L0_gnn_setup():
        import jax, jax.numpy as jnp
        import numpy as np
        ALPHA = 0.2
        EPS = 1e-05
        NEG = -9000000000000000.0
        key = jax.random.key(seed)
        k1, k2, k3, k4 = jax.random.split(key, 4)
        B, N, F_in, F_out = (8, 1024, 128, 128)
        h = jax.random.normal(k1, (B, N, F_in), dtype=jnp.float32)
        adj = jax.random.randint(k2, (B, N, N), 0, 2).astype(jnp.float32)
        W = jax.random.normal(k3, (F_in, F_out), dtype=jnp.float32) * (1.414 * np.sqrt(2.0 / (F_in + F_out)))
        a = jax.random.normal(k4, (2 * F_out, 1), dtype=jnp.float32) * (1.414 * np.sqrt(2.0 / (2 * F_out + 1)))
        gamma = jnp.ones((F_out,), dtype=jnp.float32)
        beta = jnp.zeros((F_out,), dtype=jnp.float32)
        return {'h': h, 'adj': adj, 'W': W, 'a': a, 'gamma': gamma, 'beta': beta}
    _L0_gnn_all = _L0_gnn_setup()
    _L0_gnn_in = {k: v for k, v in _L0_gnn_all.items() if k in ('W', 'a', 'gamma', 'beta')}
    del _L0_gnn_all

    def _L0_ffn_setup():
        import jax, jax.numpy as jnp
        import numpy as np
        E = 8
        K = 2
        D = 128
        H = 256
        DOUT = 128
        EPS = 1e-05
        key = jax.random.key(seed)
        ks = jax.random.split(key, 9)
        s = 0.02
        return {'x': jax.random.normal(ks[0], (4, 4096, D), jnp.float32), 'gamma': 1.0 + 0.05 * jax.random.normal(ks[1], (D,), jnp.float32), 'beta': 0.05 * jax.random.normal(ks[2], (D,), jnp.float32), 'Wr': 0.01 * jax.random.normal(ks[3], (D, E), jnp.float32), 'br': jnp.zeros((E,), jnp.float32), 'W1': s * jax.random.normal(ks[4], (E, D, H), jnp.float32), 'b1': s * jax.random.normal(ks[5], (E, H), jnp.float32), 'W2': s * jax.random.normal(ks[6], (E, H, DOUT), jnp.float32), 'b2': s * jax.random.normal(ks[7], (E, DOUT), jnp.float32)}
    _L0_ffn_all = _L0_ffn_setup()
    _L0_ffn_in = {k: v for k, v in _L0_ffn_all.items() if k in ('gamma', 'beta', 'Wr', 'br', 'W1', 'b1', 'W2', 'b2')}
    del _L0_ffn_all
    return {'x': x, 'adj': adj, 'L0_gnn_W': _L0_gnn_in['W'], 'L0_gnn_a': _L0_gnn_in['a'], 'L0_gnn_gamma': _L0_gnn_in['gamma'], 'L0_gnn_beta': _L0_gnn_in['beta'], 'L0_ffn_gamma': _L0_ffn_in['gamma'], 'L0_ffn_beta': _L0_ffn_in['beta'], 'L0_ffn_Wr': _L0_ffn_in['Wr'], 'L0_ffn_br': _L0_ffn_in['br'], 'L0_ffn_W1': _L0_ffn_in['W1'], 'L0_ffn_b1': _L0_ffn_in['b1'], 'L0_ffn_W2': _L0_ffn_in['W2'], 'L0_ffn_b2': _L0_ffn_in['b2']}

def reference(x, adj, L0_gnn_W, L0_gnn_a, L0_gnn_gamma, L0_gnn_beta, L0_ffn_gamma, L0_ffn_beta, L0_ffn_Wr, L0_ffn_br, L0_ffn_W1, L0_ffn_b1, L0_ffn_W2, L0_ffn_b2):
    import jax
    import jax.numpy as jnp

    def _L0_gnn_ref(h, adj, W, a, gamma, beta):
        import jax, jax.numpy as jnp
        import numpy as np
        ALPHA = 0.2
        EPS = 1e-05
        NEG = -9000000000000000.0
        F_out = W.shape[1]
        Wh = jnp.matmul(h, W)
        a1 = a[:F_out, 0]
        a2 = a[F_out:, 0]
        s1 = jnp.einsum('bnf,f->bn', Wh, a1)
        s2 = jnp.einsum('bnf,f->bn', Wh, a2)
        e = s1[:, :, None] + s2[:, None, :]
        e = jnp.where(e > 0, e, ALPHA * e)
        e = jnp.where(adj > 0, e, NEG)
        attention = jax.nn.softmax(e, axis=2)
        h_prime = jnp.matmul(attention, Wh)
        mu = jnp.mean(h_prime, axis=-1, keepdims=True)
        var = jnp.mean(jnp.square(h_prime - mu), axis=-1, keepdims=True)
        hn = (h_prime - mu) / jnp.sqrt(var + EPS) * gamma + beta
        return jax.nn.gelu(hn, approximate=False)

    def _L0_ffn_ref(x, gamma, beta, Wr, br, W1, b1, W2, b2):
        import jax, jax.numpy as jnp
        import numpy as np
        E = 8
        K = 2
        D = 128
        H = 256
        DOUT = 128
        EPS = 1e-05
        mu = jnp.mean(x, axis=-1, keepdims=True)
        var = jnp.mean(jnp.square(x - mu), axis=-1, keepdims=True)
        xn = (x - mu) * jax.lax.rsqrt(var + EPS) * gamma + beta
        logits = jnp.einsum('bsd,de->bse', xn, Wr) + br
        top_vals, top_idx = jax.lax.top_k(logits, K)
        w = jax.nn.softmax(top_vals, axis=-1)
        w_full = jnp.einsum('bsk,bske->bse', w, jax.nn.one_hot(top_idx, E, dtype=w.dtype))
        y = jnp.zeros(x.shape[:-1] + (DOUT,), x.dtype)
        for e in range(E):
            h = jax.nn.gelu(jnp.einsum('bsd,dh->bsh', xn, W1[e]) + b1[e], approximate=False)
            y_e = jnp.einsum('bsh,hd->bsd', h, W2[e]) + b2[e]
            y = y + y_e * w_full[..., e, None]
        return y
    x = x + _L0_gnn_ref(_layernorm(x, axis=-1), adj, L0_gnn_W, L0_gnn_a, L0_gnn_gamma, L0_gnn_beta)
    x = x + _L0_ffn_ref(_layernorm(x, axis=-1), L0_ffn_gamma, L0_ffn_beta, L0_ffn_Wr, L0_ffn_br, L0_ffn_W1, L0_ffn_b1, L0_ffn_W2, L0_ffn_b2)
    return x

_drawn_inputs = setup_inputs


def setup_inputs(seed=0):
    import zlib

    import numpy as np

    out = dict(_drawn_inputs(seed))
    spreads = {'L0_gnn_gamma': (1.0, 0.2), 'L0_gnn_beta': (0.0, 0.1), 'L0_ffn_br': (0.0, 0.307)}
    factors = {'L0_ffn_gamma': 8.0,
     'L0_ffn_beta': 8.0,
     'L0_ffn_Wr': 3.83,
     'L0_ffn_b1': 8.0,
     'L0_ffn_b2': 4.915}
    for name, (base, spread) in spreads.items():
        noise = np.random.default_rng([zlib.crc32(name.encode()), seed]).standard_normal(out[name].shape)
        drawn = base * np.exp(spread * noise) if base else spread * noise
        out[name] = jnp.asarray(drawn.astype(out[name].dtype))
    for name, factor in factors.items():
        out[name] = (out[name] * factor).astype(out[name].dtype)
    return out
```

```python
from contextlib import ExitStack

import concourse.bass as bass
from concourse import mybir

ALU = mybir.AluOpType
ACT = mybir.ActivationFunctionType
F32 = mybir.dt.float32
F32R = mybir.dt.float32r
U32 = mybir.dt.uint32
AX_X = mybir.AxisListType.X

LRELU_SLOPE = 0.2
EPS = 1e-5
NEG = -9e15
E_BASE = 2.718281828459045


class Step:

    def __init__(self, k, has, count, dma_pair):
        self.k_parity = k % 2
        self.has = has
        self.count = count
        self.dma_pair = dma_pair

    def parity(self, d):
        return (self.k_parity + d) % 2


def need(eng, sem, value):
    if isinstance(value, int) and value <= 0:
        return
    eng.wait_ge(sem, value)


def gat_moe_kernel(nc, x, adj, gnn_W, gnn_a, gnn_gamma, gnn_beta, ffn_gamma, ffn_beta,
                   Wr, br, W1, b1, W2, b2, out):
    B, N, D = x.shape
    E, _, H = W1.shape
    G = 4
    T = G * N
    NB = B // G
    HH = H // 128
    assert N == 128 and D == 128 and H == 256 and E == 8
    NHB, NWB, NHM = 3, 2, 4
    LAST = NB - 1

    def phases(k):
        return {name for name, b in (("attend", k + 2), ("route", k + 1), ("experts", k), ("finish", k - 1))
                if 0 <= b <= LAST}

    with ExitStack() as ctx:
        def sb(name, shape, dt=F32):
            return ctx.enter_context(nc.sbuf_tensor(name, shape, dt))

        def bank(name):
            return ctx.enter_context(nc.psum_tensor(name, [128, 512], F32))

        def sem(name):
            return ctx.enter_context(nc.semaphore(name))

        ident = sb("ident", [128, 128])
        ones = sb("ones", [128, 128])
        expert_ids = sb("expert_ids", [128, G, E])
        half_power = sb("half_power", [128, G])
        e_base = sb("e_base", [128, G])
        gate_rows_f = sb("gate_rows_f", [2 * E, E, 128])
        gate_rows = sb("gate_rows", [2 * E, E, 128], F32R)
        W_sb = sb("W_sb", [128, D])
        WT_sb = sb("WT_sb", [128, D])
        a_sb = sb("a_sb", [128, 2])
        a_wide = sb("a_wide", [128, 2, 128])
        Wa = sb("Wa", [128, 2, 128])
        gnn_gamma_sb = sb("gnn_gamma_sb", [128, D])
        gnn_beta_sb = sb("gnn_beta_sb", [128, D])
        ffn_gamma_sb = sb("ffn_gamma_sb", [128, 1])
        ffn_beta_sb = sb("ffn_beta_sb", [128, 1])
        Wr_sb = sb("Wr_sb", [128, E])
        br_sb = sb("br_sb", [128, E])
        W1_sb = sb("W1_sb", [128, E, H])
        W1_hi = sb("W1_hi", [128, E, H], F32R)
        W1_lo = sb("W1_lo", [128, E, H], F32R)
        W2_sb = sb("W2_sb", [128, E * HH, D])
        b1_rows = sb("b1_rows", [E * HH, 128])
        b1_sb = sb("b1_sb", [128, E * HH])
        b2_sb = sb("b2_sb", [2 * E, D])
        b2_hi = sb("b2_hi", [2 * E, D], F32R)
        b2_lo = sb("b2_lo", [2 * E, D], F32R)

        x_in = [sb(f"x_in{q}", [128, G, D]) for q in range(2)]
        adj_in = [sb(f"adj_in{q}", [128, G, N]) for q in range(2)]
        st_a = sb("st_a", [128, G, 6])
        mv_a = sb("mv_a", [128, G, 2])
        rstd_a = sb("rstd_a", [128, G])
        x_norm = sb("x_norm", [128, G, D])
        x_normT = sb("x_normT", [128, T])
        Wh = [sb(f"Wh{q}", [128, G, D]) for q in range(2)]
        score = sb("score", [128, G, N])
        mask = sb("mask", [128, G, N])
        neg_max = sb("neg_max", [128, G])
        prob = sb("prob", [128, G, N])
        prob_sum = sb("prob_sum", [128, G])
        rec_sum = [sb(f"rec_sum{q}", [128, G]) for q in range(2)]
        probT = [sb(f"probT{q}", [128, G, N]) for q in range(2)]
        st_h = sb("st_h", [128, G, 6])
        mv_h = sb("mv_h", [128, G, 2])
        rec_sq = sb("rec_sq", [128, G])
        var_h = sb("var_h", [128, G])
        rstd_h = sb("rstd_h", [128, G])
        scale_h = sb("scale_h", [128, G])
        h_norm = sb("h_norm", [128, G, D])
        h_gain = sb("h_gain", [128, G, D])
        h_affine = sb("h_affine", [128, G, D])
        h_act = sb("h_act", [128, G, D])
        x1 = [sb(f"x1_{q}", [128, G, D]) for q in range(2)]
        st_f = sb("st_f", [128, G, 6])
        mv_f = sb("mv_f", [128, G, 2])
        var_f = sb("var_f", [128, G])
        rstd_f = sb("rstd_f", [128, G])
        y_norm = sb("y_norm", [128, G, D])
        xn = sb("xn", [128, T])
        xn_hi = [sb(f"xn_hi{q}", [128, T], F32R) for q in range(2)]
        xn_lo = [sb(f"xn_lo{q}", [128, T], F32R) for q in range(2)]
        logits = sb("logits", [128, G, E])
        top = sb("top", [128, G, 8])
        top_at = sb("top_at", [128, G, 8], U32)
        top_at_f = sb("top_at_f", [128, G, 2])
        top_gap = sb("top_gap", [128, G])
        top_exp = sb("top_exp", [128, G])
        top_den = sb("top_den", [128, G])
        top_w = sb("top_w", [128, G, 2])
        pick = sb("pick", [128, 2, G, E])
        picked = sb("picked", [128, 2, G, E])
        gate = sb("gate", [128, G, E])
        gate_hl = sb("gate_hl", [128, G, 2 * E])
        gateT = [sb(f"gateT{q}", [2 * E, T], F32R) for q in range(2)]
        hid = [sb(f"hid{q}", [128, HH, T]) for q in range(2)]
        gated = [sb(f"gated{q}", [128, HH, T]) for q in range(NHM)]
        yT = sb("yT", [128, T])
        out_sb = sb("out_sb", [128, G, D])

        hid_bank = [bank(f"hid_bank{n}") for n in range(NHB)]
        gate_bank = [bank(f"gate_bank{n}") for n in range(NWB)]
        y_bank = bank("y_bank")
        bank_a = bank("bank_a")
        bank_b = bank("bank_b")

        gnn_loaded, ffn_loaded, experts_loaded = sem("gnn_loaded"), sem("ffn_loaded"), sem("experts_loaded")
        consts_ready, gate_rows_cast, setup_pe = sem("consts_ready"), sem("gate_rows_cast"), sem("setup_pe")
        ident_zero, sel_step = sem("ident_zero"), sem("sel_step")
        setup_dve, setup_act, w_split = sem("setup_dve"), sem("setup_act"), sem("w_split")
        x_loaded = [sem(f"x_loaded{q}") for q in range(2)]
        adj_loaded = [sem(f"adj_loaded{q}") for q in range(2)]
        stored = sem("stored")
        a_stats, a_aggr, a_eps, a_rstd, a_norm = (sem("a_" + n) for n in "stats aggr eps rstd norm".split())
        a_xT, a_xT_sb, a_score, a_Wh = (sem("a_" + n) for n in "xT xT_sb score Wh".split())
        a_lrelu, a_Wh_sb, a_mask, a_masked, a_max, a_prob = (
            sem("a_" + n) for n in "lrelu Wh_sb mask masked max prob".split())
        a_rec, a_probT, a_probT_sb = sem("a_rec"), sem("a_probT"), sem("a_probT_sb")
        r_h, r_sq, r_stats, r_aggr, r_var, r_eps, r_rstd, r_scale, r_norm = (
            sem("r_" + n) for n in "h sq stats aggr var eps rstd scale norm".split())
        r_gain, r_affine, r_act, r_x1, f_stats, f_aggr, f_eps, f_rstd, f_norm = (
            sem("r_" + n) for n in "gain affine act x1 stats1 aggr1 eps1 rstd1 norm1".split())
        f_yT, f_xn, f_hi, f_lo, f_logits = (sem("f_" + n) for n in "yT xn hi lo logits".split())
        g_logits, g_top, g_at, g_at_f, g_gap, g_exp, g_den, g_w1, g_w2, g_pick, g_picked, g_gate, g_hi, g_lo = (
            sem("g_" + n) for n in "logits top at at_f gap exp den w1 w2 pick picked gate hi lo".split())
        g_T, g_T_sb = sem("g_T"), sem("g_T_sb")
        up = [sem(f"up{n}") for n in range(E * HH)]
        act = [sem(f"act{n}") for n in range(E * HH)]
        spread = [sem(f"spread{e}") for e in range(E)]
        gated_ok = [sem(f"gated_ok{e}") for e in range(E)]
        down = [sem(f"down{e}") for e in range(E)]
        o_yT, o_y, o_sum = sem("o_yT"), sem("o_y"), sem("o_sum")

        uses = E * HH
        bank_before = []
        for n in range(uses):
            earlier = [m for m in range(n) if m % NHB == n % NHB]
            bank_before.append((earlier[-1], False) if earlier else
                               (max(m for m in range(uses) if m % NHB == n % NHB), True))

        block = ctx.enter_context(nc.Block())

        def run(eng, step, first, loop_from, loop_to, last, dma_pairs=()):
            for k in range(first, loop_from):
                step(Step(k, phases(k), lambda d, k=k: k + d, lambda d, k=k: 16 * (k // 2 + d)))
            with eng.Fori(0, (loop_to - loop_from) // 2) as i:
                base = 2 * i + loop_from
                value = {d: eng.snap(eng.to_reg(base + d)) for d in range(-1, 5)}
                pair = {d: eng.snap(eng.to_reg(16 * i + 16 * (loop_from // 2 + d))) for d in dma_pairs}
                for u in range(2):
                    step(Step(loop_from + u, phases(loop_from + u), lambda d, u=u: value[u + d],
                              lambda d: pair[d]))
            for k in range(loop_to, last + 1):
                step(Step(k, phases(k), lambda d, k=k: k + d, lambda d, k=k: 16 * (k // 2 + d)))

        @block.sync
        def _(sp):
            xv = x.rearrange("b t f -> t b f")
            av = adj.rearrange("b t f -> t b f")
            ov = out.rearrange("b t f -> t b f")

            def load(b_count, row, q, early=None):
                sp.wait_ge(gnn_loaded, 16)
                need(sp, r_x1, b_count)
                need(sp, a_mask, b_count)
                sp.dma_start(x_in[q][:, :, :], xv[:, row, :]).then_inc(x_loaded[q], 16)
                sp.dma_start(adj_in[q][:, :, :], av[:, row, :]).then_inc(adj_loaded[q], 16)

            sp.dma_start(x_in[0][:, :, :], xv[:, 0:G, :]).then_inc(x_loaded[0], 16)
            sp.dma_start(adj_in[0][:, :, :], av[:, 0:G, :]).then_inc(adj_loaded[0], 16)
            sp.dma_start(W_sb[:, :], gnn_W).then_inc(gnn_loaded, 16)
            for r in range(2):
                sp.dma_start(a_sb[:, r:r + 1], gnn_a[r * D:(r + 1) * D, :]).then_inc(gnn_loaded, 16)
            sp.dma_start(gnn_gamma_sb[:, :], gnn_gamma.partition_broadcast(128)).then_inc(gnn_loaded, 16)
            sp.dma_start(gnn_beta_sb[:, :], gnn_beta.partition_broadcast(128)).then_inc(gnn_loaded, 16)
            sp.dma_start(x_in[1][:, :, :], xv[:, G:2 * G, :]).then_inc(x_loaded[1], 16)
            sp.dma_start(adj_in[1][:, :, :], av[:, G:2 * G, :]).then_inc(adj_loaded[1], 16)
            sp.dma_start(W1_sb[:, :, :], W1.rearrange("e k h -> k e h")).then_inc(experts_loaded, 16)
            sp.dma_start(W2_sb[:, :, :], W2.rearrange("e (a p) d -> p (e a) d", p=128)).then_inc(experts_loaded, 16)

            def store(s, row):
                sp.wait_ge(gnn_loaded, 16)
                need(sp, o_sum, s.count(0))
                sp.dma_start(ov[:, row, :], out_sb[:, :, :]).then_inc(stored, 16)

            for k in range(-1, 2):
                if k == 1:
                    store(Step(k, phases(k), lambda d: 1 + d, None), slice(0, G))
                load(k + 2, slice((k + 3) * G, (k + 4) * G), (k + 3) % 2)
            with sp.Fori(0, (LAST - 5) // 2) as i:
                value = {d: sp.snap(sp.to_reg(2 * i + 2 + d)) for d in (0, 1, 2, 3)}
                for u in range(2):
                    store(Step(u, (), lambda d, u=u: value[u + d], None), bass.ds((2 * i + 1 + u) * G, G))
                    load(value[u + 2], bass.ds((2 * i + 5 + u) * G, G), (u + 1) % 2)
            for k in range(2 + 2 * ((LAST - 5) // 2), NB + 1):
                store(Step(k, (), lambda d, k=k: k + d, None), slice((k - 1) * G, k * G))
                if k + 3 <= LAST:
                    load(k + 2, slice((k + 3) * G, (k + 4) * G), (k + 3) % 2)
            sp.wait_ge(stored, 16 * NB)

        @block.gpsimd
        def _(pool):
            g = nc.gpsimd
            g.memset(ident[:, :], 0.0).then_inc(ident_zero, 1)
            g.memset(gate_rows_f[:, :, :], 0.0).then_inc(ident_zero, 1)
            pool.wait_ge(ident_zero, 2)
            g.affine_select(out=ident[:, :], in_=ident[:, :], compare_op=ALU.not_equal, fill=1.0,
                            base=0, pattern=[[-1, 128]], channel_multiplier=1).then_inc(consts_ready, 1)
            g.affine_select(out=gate_rows_f[:, :, :], in_=gate_rows_f[:, :, :], compare_op=ALU.not_equal, fill=1.0,
                            base=0, pattern=[[-1, E], [0, 128]], channel_multiplier=1).then_inc(sel_step, 1)
            pool.wait_ge(sel_step, 1)
            g.affine_select(out=gate_rows_f[:, :, :], in_=gate_rows_f[:, :, :], compare_op=ALU.not_equal, fill=1.0,
                            base=-E, pattern=[[-1, E], [0, 128]], channel_multiplier=1).then_inc(sel_step, 1)
            g.memset(half_power[:, :], -0.5).then_inc(consts_ready, 1)
            g.memset(e_base[:, :], E_BASE).then_inc(consts_ready, 1)
            for e in range(E):
                g.memset(expert_ids[:, :, e:e + 1], float(e)).then_inc(consts_ready, 1)
            pool.wait_ge(sel_step, 2)
            g.tensor_copy(gate_rows[:, :, :], gate_rows_f[:, :, :]).then_inc(gate_rows_cast, 1)
            pool.wait_ge(consts_ready, 3 + E)
            pool.wait_ge(gnn_loaded, 80)

            def step(s):
                c, has = s.count, s.has
                if "attend" in has:
                    pool.wait_ge(consts_ready, 3)
                    need(pool, a_aggr, c(3))
                    need(pool, a_norm, c(2))
                    g.tensor_scalar(rstd_a[:, :], mv_a[:, :, 1], EPS, 1.0, ALU.add, ALU.mult).then_inc(a_eps, 1)
                    need(pool, a_eps, c(3))
                    g.tensor_tensor(rstd_a[:, :], rstd_a[:, :], half_power[:, :], ALU.pow).then_inc(a_rstd, 1)
                if "route" in has:
                    q = s.parity(1)
                    need(pool, a_rec, c(2))
                    need(pool, r_var, c(1))
                    g.tensor_tensor(rec_sq[:, :], rec_sum[q][:, :], rec_sum[q][:, :], ALU.mult).then_inc(r_sq, 1)
                    need(pool, r_aggr, c(2))
                    need(pool, r_sq, c(2))
                    need(pool, r_rstd, c(1))
                    g.tensor_tensor(var_h[:, :], mv_h[:, :, 1], rec_sq[:, :], ALU.mult).then_inc(r_var, 1)
                    pool.wait_ge(consts_ready, 3)
                    need(pool, r_var, c(2))
                    g.tensor_scalar(rstd_h[:, :], var_h[:, :], EPS, 1.0, ALU.add, ALU.mult).then_inc(r_eps, 1)
                    need(pool, r_eps, c(2))
                    g.tensor_tensor(rstd_h[:, :], rstd_h[:, :], half_power[:, :], ALU.pow).then_inc(r_rstd, 1)
                    need(pool, r_rstd, c(2))
                    need(pool, r_norm, c(1))
                    g.tensor_tensor(scale_h[:, :], rstd_h[:, :], rec_sum[q][:, :], ALU.mult).then_inc(r_scale, 1)
                    need(pool, r_norm, c(2))
                    need(pool, r_affine, c(1))
                    g.tensor_tensor(h_gain[:, :, :], h_norm[:, :, :],
                                    gnn_gamma_sb[:, :].unsqueeze(1).to_broadcast([128, G, D]),
                                    ALU.mult).then_inc(r_gain, 1)
                    need(pool, r_gain, c(2))
                    need(pool, r_act, c(1))
                    g.tensor_tensor(h_affine[:, :, :], h_gain[:, :, :],
                                    gnn_beta_sb[:, :].unsqueeze(1).to_broadcast([128, G, D]),
                                    ALU.add).then_inc(r_affine, 1)
                    need(pool, r_act, c(2))
                    need(pool, o_sum, c(0))
                    g.tensor_tensor(x1[q][:, :, :], x_in[q][:, :, :], h_act[:, :, :], ALU.add).then_inc(r_x1, 1)
                    pool.wait_ge(consts_ready, 3)
                    need(pool, f_aggr, c(2))
                    need(pool, f_norm, c(1))
                    g.tensor_scalar(rstd_f[:, :], mv_f[:, :, 1], 1.0 + EPS, EPS * EPS,
                                    ALU.mult, ALU.add).then_inc(f_eps, 1)
                    need(pool, f_eps, c(2))
                    g.tensor_tensor(rstd_f[:, :], rstd_f[:, :], half_power[:, :], ALU.pow).then_inc(f_rstd, 1)
                    need(pool, f_hi, c(2))
                    need(pool, up[uses - 1], c(0))
                    g.tensor_tensor(xn_lo[q][:, :], xn[:, :], xn_hi[q][:, :].bitcast(F32),
                                    ALU.subtract).then_inc(f_lo, 1)
                    need(pool, g_gap, c(2))
                    need(pool, g_w2, c(1))
                    g.tensor_tensor(top_exp[:, :], e_base[:, :], top_gap[:, :], ALU.pow).then_inc(g_exp, 1)

            run(pool, step, -2, 2, 2 + 2 * ((LAST - 3) // 2), NB)

        @block.scalar
        def _(scalar):
            a = nc.scalar
            scalar.dma_start(ffn_gamma_sb[:, :], ffn_gamma.unsqueeze(1)).then_inc(ffn_loaded, 16)
            scalar.dma_start(ffn_beta_sb[:, :], ffn_beta.unsqueeze(1)).then_inc(ffn_loaded, 16)
            scalar.dma_start(Wr_sb[:, :], Wr).then_inc(ffn_loaded, 16)
            scalar.dma_start(br_sb[:, :], br.partition_broadcast(128)).then_inc(ffn_loaded, 16)
            scalar.dma_start(b1_rows[:, :], b1.rearrange("e (a p) -> (e a) p", p=128)).then_inc(ffn_loaded, 16)
            for r in range(2):
                scalar.dma_start(b2_sb[r * E:(r + 1) * E, :], b2).then_inc(ffn_loaded, 16)
            scalar.wait_ge(setup_pe, 1)
            a.copy(WT_sb[:, :], bank_a[:, 0:D]).then_inc(setup_act, 1)
            scalar.wait_ge(setup_pe, 2)
            a.copy(Wa[:, :, :], bank_b[:, 0:256].rearrange("p (s n) -> p s n", s=2)).then_inc(setup_act, 1)
            scalar.wait_ge(setup_pe, 3)
            a.copy(b1_sb[:, :], bank_a[:, 0:uses]).then_inc(setup_act, 1)
            scalar.wait_ge(ffn_loaded, 16 * 7)

            def gelu_expert(s, n):
                e, h = divmod(n, HH)
                need(scalar, up[n], s.count(1))
                need(scalar, gated_ok[(e - 2) % E], s.count(1 if e >= 2 else 0))
                a.activation(hid[e % 2][:, h, :], hid_bank[n % NHB][:, :], ACT.Gelu,
                             bias=b1_sb[:, n:n + 1]).then_inc(act[n], 1)

            def step(s):
                c, has = s.count, s.has
                q1, q2 = s.parity(1), s.parity(2)
                for e in range(E):
                    if e == 1 and "finish" in has:
                        need(scalar, down[E - 1], c(0))
                        need(scalar, o_y, c(-1))
                        a.copy(yT[:, :], y_bank[:, :]).then_inc(o_yT, 1)
                    if e == 2 and "attend" in has:
                        need(scalar, a_xT, c(3))
                        need(scalar, a_Wh, c(2))
                        a.copy(x_normT[:, :], bank_a[:, :]).then_inc(a_xT_sb, 1)
                    if e == 3 and "route" in has:
                        need(scalar, r_affine, c(2))
                        need(scalar, r_x1, c(1))
                        a.activation(h_act[:, :, :], h_affine[:, :, :], ACT.Gelu).then_inc(r_act, 1)
                    if e == 4 and "attend" in has:
                        need(scalar, a_Wh, c(3))
                        need(scalar, r_h, c(1))
                        a.copy(Wh[q2][:, :, :], bank_b[:, :].rearrange("p (g n) -> p g n", g=G)).then_inc(a_Wh_sb, 1)
                    if e == 5 and "route" in has:
                        need(scalar, f_yT, c(2))
                        need(scalar, f_logits, c(1))
                        need(scalar, f_lo, c(1))
                        a.activation(xn[:, :], bank_a[:, :], ACT.Identity, bias=ffn_beta_sb[:, :],
                                     scale=ffn_gamma_sb[:, :]).then_inc(f_xn, 1)
                        need(scalar, up[uses - 1], c(0))
                        a.activation(xn_hi[q1][:, :], bank_a[:, :], ACT.Identity, bias=ffn_beta_sb[:, :],
                                     scale=ffn_gamma_sb[:, :]).then_inc(f_hi, 1)
                    if e == 6 and "attend" in has:
                        need(scalar, a_max, c(3))
                        need(scalar, a_probT, c(2))
                        need(scalar, a_rec, c(2))
                        for j in range(G):
                            ins = a.activation(prob[:, j, :], score[:, j, :], ACT.Exp, bias=neg_max[:, j:j + 1],
                                               accum_out=prob_sum[:, j:j + 1])
                        ins.then_inc(a_prob, 1)
                    if "experts" in has:
                        for h in range(HH):
                            gelu_expert(s, e * HH + h)
                    if e == 7 and "attend" in has:
                        need(scalar, a_probT, c(3))
                        need(scalar, r_h, c(1))
                        a.copy(probT[q2][:, :, :],
                               bank_a[:, :].rearrange("p (g n) -> p g n", g=G)).then_inc(a_probT_sb, 1)
                if "route" in has:
                    need(scalar, g_T, c(2))
                    need(scalar, spread[E - 1], c(0))
                    a.copy(gateT[q1][:, :], bank_b[0:2 * E, :]).then_inc(g_T_sb, 1)

            run(scalar, step, -2, 2, 2 + 2 * ((LAST - 3) // 2), NB)

        @block.vector
        def _(dve):
            v = nc.vector
            dve.wait_ge(consts_ready, 3 + E)
            v.memset(ones[:, :], 1.0).then_inc(setup_dve, 1)
            dve.wait_ge(gnn_loaded, 80)
            dve.wait_ge(setup_dve, 1)
            for r in range(2):
                v.tensor_scalar(a_wide[:, r, :], ones[:, :], a_sb[:, r:r + 1], None, ALU.mult).then_inc(setup_dve, 1)
            dve.wait_ge(ffn_loaded, 16 * 7)

            def split_parameters():
                dve.wait_ge(experts_loaded, 32)
                v.tensor_copy(W1_hi[:, :, :], W1_sb[:, :, :]).then_inc(w_split, 1)
                v.tensor_copy(b2_hi[:, :], b2_sb[:, :]).then_inc(w_split, 1)
                dve.wait_ge(w_split, 2)
                v.tensor_tensor(W1_lo[:, :, :], W1_sb[:, :, :], W1_hi[:, :, :].bitcast(F32),
                                ALU.subtract).then_inc(w_split, 1)
                v.tensor_tensor(b2_lo[:, :], b2_sb[:, :], b2_hi[:, :].bitcast(F32),
                                ALU.subtract).then_inc(w_split, 1)

            def norm_stats(src, st, mv, stats_done, aggr_done, value):
                for j in range(G):
                    ins = v.bn_stats(st[:, j, :], src[j])
                ins.then_inc(stats_done, 1)
                dve.wait_ge(consts_ready, 1)
                need(dve, stats_done, value)
                for j in range(G):
                    ins = v.bn_aggr(mv[:, j, :], st[:, j, :])
                ins.then_inc(aggr_done, 1)

            def gate_hidden(s, e):
                need(dve, act[e * HH + HH - 1], s.count(1))
                need(dve, spread[e], s.count(1))
                need(dve, down[(e - NHM) % E], s.count(1 if e >= NHM else 0))
                v.tensor_tensor(gated[e % NHM][:, :, :], hid[e % 2][:, :, :],
                                gate_bank[e % NWB][:, :].unsqueeze(1).to_broadcast([128, HH, T]),
                                ALU.mult).then_inc(gated_ok[e], 1)

            def per_graph(ap):
                return [ap[:, j * D:(j + 1) * D] for j in range(G)]

            def step(s):
                c, has = s.count, s.has
                q0, q1, q2 = s.parity(0), s.parity(1), s.parity(2)
                for e in range(E):
                    if e == 0 and "attend" in has:
                        need(dve, x_loaded[q2], s.dma_pair(2))
                        need(dve, a_rstd, c(2))
                        norm_stats([x_in[q2][:, j, :] for j in range(G)], st_a, mv_a, a_stats, a_aggr, c(3))
                    if e == 0 and "route" in has:
                        need(dve, r_h, c(2))
                        need(dve, r_norm, c(1))
                        norm_stats(per_graph(bank_b), st_h, mv_h, r_stats, r_aggr, c(2))
                    if e == 0 and "attend" in has:
                        need(dve, a_rstd, c(3))
                        need(dve, a_xT, c(2))
                        for j in range(G):
                            ins = v.tensor_scalar(x_norm[:, j, :], x_in[q2][:, j, :], mv_a[:, j, 0:1],
                                                  rstd_a[:, j:j + 1], ALU.subtract, ALU.mult)
                        ins.then_inc(a_norm, 1)
                    if e == 1 and "route" in has:
                        need(dve, r_scale, c(2))
                        need(dve, r_gain, c(1))
                        for j in range(G):
                            ins = v.tensor_scalar(h_norm[:, j, :], per_graph(bank_b)[j], mv_h[:, j, 0:1],
                                                  scale_h[:, j:j + 1], ALU.subtract, ALU.mult)
                        ins.then_inc(r_norm, 1)
                    if e == 2 and "attend" in has:
                        need(dve, adj_loaded[q2], s.dma_pair(2))
                        need(dve, a_prob, c(2))
                        v.tensor_scalar(mask[:, :, :], adj_in[q2][:, :, :], 0.0, NEG / LRELU_SLOPE,
                                        ALU.is_le, ALU.mult).then_inc(a_mask, 1)
                    if e == 3 and "finish" in has:
                        need(dve, o_y, c(0))
                        need(dve, stored, s.stored)
                        v.tensor_tensor(out_sb[:, :, :], bank_b[:, :].rearrange("p (g n) -> p g n", g=G),
                                        x1[s.parity(-1)][:, :, :], ALU.add).then_inc(o_sum, 1)
                    if e == 3 and "route" in has:
                        need(dve, r_x1, c(2))
                        need(dve, f_rstd, c(1))
                        norm_stats([x1[q1][:, j, :] for j in range(G)], st_f, mv_f, f_stats, f_aggr, c(2))
                        need(dve, f_rstd, c(2))
                        need(dve, f_yT, c(1))
                        for j in range(G):
                            ins = v.tensor_scalar(y_norm[:, j, :], x1[q1][:, j, :], mv_f[:, j, 0:1],
                                                  rstd_f[:, j:j + 1], ALU.subtract, ALU.mult)
                        ins.then_inc(f_norm, 1)
                    if e == 4 and "attend" in has:
                        need(dve, a_score, c(3))
                        need(dve, a_mask, c(3))
                        v.tensor_tensor(mask[:, :, :], bank_a[:, :].rearrange("p (g n) -> p g n", g=G),
                                        mask[:, :, :], ALU.add).then_inc(a_masked, 1)
                        need(dve, a_masked, c(3))
                        v.scalar_tensor_tensor(score[:, :, :], mask[:, :, :], LRELU_SLOPE, mask[:, :, :],
                                               ALU.mult, ALU.max).then_inc(a_lrelu, 1)
                        need(dve, a_lrelu, c(3))
                        v.tensor_reduce(neg_max[:, :], score[:, :, :], AX_X, ALU.max, negate=True).then_inc(a_max, 1)
                    if e == 6 and "route" in has:
                        need(dve, f_logits, c(2))
                        v.tensor_tensor(logits[:, :, :],
                                        bank_b[:, 0:G * E].rearrange("p (g e) -> p g e", g=G),
                                        br_sb[:, :].unsqueeze(1).to_broadcast([128, G, E]),
                                        ALU.add).then_inc(g_logits, 1)
                        dve.wait_ge(consts_ready, 1)
                        need(dve, g_logits, c(2))
                        for j in range(G):
                            ins = v.max(top[:, j, :], logits[:, j, :])
                        ins.then_inc(g_top, 1)
                        dve.wait_ge(consts_ready, 1)
                        need(dve, g_top, c(2))
                        for j in range(G):
                            ins = v.max_index(top_at[:, j, :], top[:, j, :], logits[:, j, :])
                        ins.then_inc(g_at, 1)
                        v.tensor_tensor(top_gap[:, :], top[:, :, 1], top[:, :, 0], ALU.subtract).then_inc(g_gap, 1)
                        need(dve, g_at, c(2))
                        v.tensor_copy(top_at_f[:, :, :], top_at[:, :, 0:2]).then_inc(g_at_f, 1)
                        need(dve, g_at_f, c(2))
                        for r in range(2):
                            ins = v.tensor_tensor(pick[:, r, :, :], expert_ids[:, :, :],
                                                  top_at_f[:, :, r:r + 1].to_broadcast([128, G, E]), ALU.is_equal)
                        ins.then_inc(g_pick, 1)
                        need(dve, g_exp, c(2))
                        v.tensor_scalar(top_den[:, :], top_exp[:, :], 1.0, None, ALU.add).then_inc(g_den, 1)
                        need(dve, g_den, c(2))
                        v.reciprocal(top_w[:, :, 0], top_den[:, :]).then_inc(g_w1, 1)
                        need(dve, g_w1, c(2))
                        v.tensor_tensor(top_w[:, :, 1], top_w[:, :, 0], top_exp[:, :], ALU.mult).then_inc(g_w2, 1)
                        need(dve, g_w2, c(2))
                        for r in range(2):
                            ins = v.tensor_tensor(picked[:, r, :, :], pick[:, r, :, :],
                                                  top_w[:, :, r:r + 1].to_broadcast([128, G, E]), ALU.mult)
                        ins.then_inc(g_picked, 1)
                        need(dve, g_picked, c(2))
                        v.tensor_tensor(gate[:, :, :], picked[:, 0, :, :], picked[:, 1, :, :],
                                        ALU.add).then_inc(g_gate, 1)
                        need(dve, g_gate, c(2))
                        need(dve, g_T, c(1))
                        v.tensor_copy(gate_hl[:, :, 0:E].bitcast(F32R), gate[:, :, :]).then_inc(g_hi, 1)
                        need(dve, g_hi, c(2))
                        v.tensor_tensor(gate_hl[:, :, E:2 * E], gate[:, :, :], gate_hl[:, :, 0:E],
                                        ALU.subtract).then_inc(g_lo, 1)
                    if e == 7 and "attend" in has:
                        need(dve, a_prob, c(3))
                        need(dve, r_scale, c(1))
                        v.reciprocal(rec_sum[q2][:, :], prob_sum[:, :]).then_inc(a_rec, 1)
                    if "experts" in has:
                        gate_hidden(s, e)

            def first(k):
                s = Step(k, phases(k), lambda d: k + d, lambda d: 16 * (k // 2 + d))
                s.stored = 16 * (k - 1)
                step(s)

            for k in (-2, -1):
                first(k)
            split_parameters()
            for k in (0, 1):
                first(k)
            loops = (LAST - 3) // 2
            with dve.Fori(0, loops) as i:
                value = {d: dve.snap(dve.to_reg(2 * i + 2 + d)) for d in range(0, 5)}
                pair = {2: dve.snap(dve.to_reg(16 * i + 16 * 3))}
                stored_value = [dve.snap(dve.to_reg(32 * i + 16 * (1 + u))) for u in range(2)]
                for u in range(2):
                    s = Step(2 + u, phases(2 + u), lambda d, u=u: value[u + d], lambda d: pair[d])
                    s.stored = stored_value[u]
                    step(s)
            for k in range(2 + 2 * loops, NB + 1):
                first(k)

        @block.tensor
        def _(pe):
            t = nc.tensor
            pe.wait_ge(consts_ready, 1)
            pe.wait_ge(gnn_loaded, 80)
            t.transpose(bank_a[:, 0:D], W_sb[:, :], ident[:, :]).then_inc(setup_pe, 1)
            pe.wait_ge(setup_act, 1)
            pe.wait_ge(setup_dve, 3)
            for r in range(2):
                ins = t.matmul(bank_b[:, 128 * r:128 * r + 128], WT_sb[:, :], a_wide[:, r, :],
                               start=(r == 0), stop=True, skip_group_check=True)
            ins.then_inc(setup_pe, 1)
            pe.wait_ge(ffn_loaded, 16 * 7)
            t.transpose(bank_a[:, 0:uses], b1_rows[:, :], ident[0:uses, 0:uses]).then_inc(setup_pe, 1)
            pe.wait_ge(setup_act, 3)

            def second_product(e, b_value):
                need(pe, gated_ok[e], b_value)
                for h in range(HH):
                    ins = t.matmul(y_bank[:, :], W2_sb[:, e * HH + h, :], gated[e % NHM][:, h, :],
                                   start=False, stop=(e == E - 1 and h == HH - 1), skip_group_check=True)
                ins.then_inc(down[e], 1)

            def bias_product(s):
                q = s.parity(0)
                need(pe, o_yT, s.count(0))
                t.matmul(y_bank[:, :], b2_hi[:, :], gateT[q][:, :], start=True, stop=False, skip_group_check=True)
                t.matmul(y_bank[:, :], b2_lo[:, :], gateT[q][:, :], start=False, stop=False, skip_group_check=True)

            def first_product(s, e):
                q = s.parity(0)
                for h in range(HH):
                    n = e * HH + h
                    before, wrapped = bank_before[n]
                    need(pe, act[before], s.count(0 if wrapped else 1))
                    cols = slice(h * 128, h * 128 + 128)
                    dst = hid_bank[n % NHB][:, :]
                    t.matmul(dst, W1_hi[:, e, cols], xn_lo[q][:, :], start=True, stop=False)
                    t.matmul(dst, W1_lo[:, e, cols], xn_hi[q][:, :], start=False, stop=False)
                    t.matmul(dst, W1_hi[:, e, cols], xn_hi[q][:, :], start=False, stop=True).then_inc(up[n], 1)

            def spread_gate(s, e):
                need(pe, gated_ok[(e - NWB) % E], s.count(1 if e >= NWB else 0))
                t.matmul(gate_bank[e % NWB][:, :], gate_rows[:, e, :], gateT[s.parity(0)][:, :],
                         start=True, stop=True).then_inc(spread[e], 1)

            def transposes(dst, src, width=128):
                for j in range(G):
                    ins = t.transpose(dst[0:width, j * 128:j * 128 + 128], src[j], ident[:, :])
                return ins

            def step(s):
                c, has = s.count, s.has
                q0, q1, q2 = s.parity(0), s.parity(1), s.parity(2)
                for e in range(E):
                    if e < 2 and "finish" in has:
                        second_product(E - 2 + e, c(0))
                    if e >= 2 and "experts" in has:
                        if e == 2:
                            bias_product(s)
                        second_product(e - 2, c(1))
                    if "experts" in has:
                        if e == 0:
                            need(pe, f_lo, c(1))
                            need(pe, g_T_sb, c(1))
                        first_product(s, e)
                        spread_gate(s, e)
                    if e == 0 and "route" in has:
                        need(pe, a_probT_sb, c(2))
                        need(pe, a_Wh_sb, c(2))
                        need(pe, g_T_sb, c(1))
                        for j in range(G):
                            ins = t.matmul(bank_b[:, j * D:(j + 1) * D], probT[q1][:, j, :], Wh[q1][:, j, :],
                                           start=True, stop=True)
                        ins.then_inc(r_h, 1)
                    if e == 1 and "attend" in has:
                        need(pe, a_norm, c(3))
                        need(pe, a_probT_sb, c(2))
                        transposes(bank_a, [x_norm[:, j, :] for j in range(G)]).then_inc(a_xT, 1)
                    if e == 2 and "finish" in has:
                        need(pe, o_yT, c(0))
                        need(pe, r_norm, c(2) if "route" in has else NB)
                        transposes(bank_b, [yT[:, j * N:(j + 1) * N] for j in range(G)]).then_inc(o_y, 1)
                    if e == 3 and "attend" in has:
                        need(pe, a_xT_sb, c(3))
                        t.matmul(bank_a[:, :], Wa[:, 1, :], x_normT[:, :], start=True, stop=False,
                                 skip_group_check=True)
                        for j in range(G):
                            cols = slice(j * N, (j + 1) * N)
                            ins = t.matmul(bank_a[:, cols], x_normT[:, cols], Wa[:, 0, :], start=False, stop=True,
                                           skip_group_check=True)
                        ins.then_inc(a_score, 1)
                        need(pe, o_sum, c(0))
                        need(pe, r_norm, c(2))
                        for j in range(G):
                            ins = t.matmul(bank_b[:, j * D:(j + 1) * D], x_normT[:, j * N:(j + 1) * N], W_sb[:, :],
                                           start=True, stop=True)
                        ins.then_inc(a_Wh, 1)
                    if e == 4 and "route" in has:
                        need(pe, f_norm, c(2))
                        need(pe, a_masked, c(3) if "attend" in has else c(2))
                        transposes(bank_a, [y_norm[:, j, :] for j in range(G)]).then_inc(f_yT, 1)
                    if e == 5 and "route" in has:
                        need(pe, f_xn, c(2))
                        need(pe, a_Wh_sb, c(3) if "attend" in has else c(2))
                        need(pe, o_sum, c(0))
                        for j in range(G):
                            ins = t.matmul(bank_b[:, j * E:(j + 1) * E], xn[:, j * N:(j + 1) * N], Wr_sb[:, :],
                                           start=True, stop=True)
                        ins.then_inc(f_logits, 1)
                    if e == 6 and "attend" in has:
                        need(pe, a_prob, c(3))
                        need(pe, f_hi, c(2))
                        transposes(bank_a, [prob[:, j, :] for j in range(G)]).then_inc(a_probT, 1)
                    if e == 7 and "route" in has:
                        need(pe, g_lo, c(2))
                        need(pe, g_logits, c(2))
                        transposes(bank_b, [gate_hl[:, j, :] for j in range(G)], 2 * E).then_inc(g_T, 1)

            loops = (LAST - 3) // 2
            def whole(k):
                if k == 0:
                    pe.wait_ge(w_split, 4)
                    pe.wait_ge(gate_rows_cast, 1)
                step(Step(k, phases(k), lambda d: k + d, None))
            for k in range(-2, 2):
                whole(k)
            with pe.Fori(0, loops) as i:
                value = {d: pe.snap(pe.to_reg(2 * i + 2 + d)) for d in range(0, 5)}
                for u in range(2):
                    step(Step(2 + u, phases(2 + u), lambda d, u=u: value[u + d], None))
            for k in range(2 + 2 * loops, NB + 1):
                whole(k)


_INS = ["x", "adj", "L0_gnn_W", "L0_gnn_a", "L0_gnn_gamma", "L0_gnn_beta", "L0_ffn_gamma", "L0_ffn_beta",
        "L0_ffn_Wr", "L0_ffn_br", "L0_ffn_W1", "L0_ffn_b1", "L0_ffn_W2", "L0_ffn_b2"]


def kernel(**inputs):
    import numpy as np
    import concourse.bacc as bacc
    from concourse.bass_utils import run_bass_kernel_spmd

    nc = bacc.Bacc("TRN2", target_bir_lowering=False, num_devices=1)
    arrays, args = {}, []
    for name in _INS:
        arr = np.ascontiguousarray(inputs[name])
        arrays[name + "_dram"] = arr
        args.append(nc.dram_tensor(name + "_dram", arr.shape, mybir.dt.from_np(arr.dtype), kind="ExternalInput").ap())
    shape = inputs["x"].shape
    args.append(nc.dram_tensor("out_dram", shape, F32, kind="ExternalOutput").ap())
    gat_moe_kernel(nc, *args)
    r = run_bass_kernel_spmd(nc, [arrays], core_ids=[0])
    return r.results[0]["out_dram"]
```

```python
from contextlib import ExitStack

import concourse.bass as bass
from concourse import mybir

ALU = mybir.AluOpType
ACT = mybir.ActivationFunctionType
F32 = mybir.dt.float32
F32R = mybir.dt.float32r
U32 = mybir.dt.uint32
AX_X = mybir.AxisListType.X

LRELU_SLOPE = 0.2
EPS = 1e-5
NEG = -9e15
E_BASE = 2.718281828459045


class Step:

    def __init__(self, k, blocks, count, loads):
        self.k = k
        self.blocks = blocks
        self.count = count
        self.loads = loads

    def has(self, d):
        return self.blocks is None or 0 <= self.k + d < self.blocks

    def parity(self, d):
        return (self.k + d) % 2


def need(eng, sem, value):
    if isinstance(value, int) and value <= 0:
        return
    eng.wait_ge(sem, value)


def gat_moe_kernel(nc, x, adj, gnn_W, gnn_a, gnn_gamma, gnn_beta, ffn_gamma, ffn_beta,
                   Wr, br, W1, b1, W2, b2, out):
    B, N, D = x.shape
    E, _, H = W1.shape
    G = 4
    T = G * N
    NB = B // G
    HH = H // 128
    assert N == 128 and D == 128 and H == 256 and E == 8
    NHB, NYB = 3, 2
    LAG = 2
    NH = 4
    BIAS_SLOT = 5
    BIAS_EXPERT = 4
    GE = G * E
    FIRST_STEP, LAST_STEP = -3, NB
    LOOP_FROM, LOOP_TO = 2, 2 + (NB - 5) // 2 * 2

    with ExitStack() as ctx:
        def sb(name, shape, dt=F32):
            return ctx.enter_context(nc.sbuf_tensor(name, shape, dt))

        def bank(name):
            return ctx.enter_context(nc.psum_tensor(name, [128, 512], F32))

        def sem(name):
            return ctx.enter_context(nc.semaphore(name))

        ident = sb("ident", [128, 128])
        expert_ids = sb("expert_ids", [128, G, E])
        half_power = sb("half_power", [128, G])
        e_base = sb("e_base", [128, G])
        W_ext = sb("W_ext", [128, D + 2])
        WT_sb = sb("WT_sb", [128, D])
        a_sb = sb("a_sb", [128, 2])
        gnn_gamma_sb = sb("gnn_gamma_sb", [128, D])
        gnn_beta_sb = sb("gnn_beta_sb", [128, D])
        ffn_gamma_sb = sb("ffn_gamma_sb", [128, 1])
        ffn_beta_sb = sb("ffn_beta_sb", [128, 1])
        Wr_sb = sb("Wr_sb", [128, E])
        br_sb = sb("br_sb", [128, E])
        W1_sb = sb("W1_sb", [128, E, H])
        W1_hi = sb("W1_hi", [128, E, H], F32R)
        W1_lo = sb("W1_lo", [128, E, H], F32R)
        W2_sb = sb("W2_sb", [128, E * HH, D])
        b1_rows = sb("b1_rows", [E * HH, 128])
        b1_sb = sb("b1_sb", [128, E * HH])
        b2_blocks = sb("b2_blocks", [3 * GE, G, D])
        b2_hi = sb("b2_hi", [3 * GE, G, D], F32R)
        b2_parts = sb("b2_parts", [3 * GE, G, D], F32R)

        x_in = [sb(f"x_in{q}", [128, G, D]) for q in range(2)]
        adj_in = [sb(f"adj_in{q}", [128, G, N]) for q in range(2)]
        st_a = sb("st_a", [128, G, 6])
        mv_a = sb("mv_a", [128, G, 2])
        rstd_a = sb("rstd_a", [128, G])
        x_norm = sb("x_norm", [128, G, D])
        x_normT = sb("x_normT", [128, T])
        Wh = sb("Wh", [128, G, D + 2])
        score = sb("score", [128, G, N])
        mask = sb("mask", [128, G, N])
        neg_max = sb("neg_max", [128, G])
        prob = sb("prob", [128, G, N])
        prob_sum = sb("prob_sum", [128, G])
        rec_sum = sb("rec_sum", [128, G])
        probT = sb("probT", [128, G, N])
        st_h = sb("st_h", [128, G, 6])
        mv_h = sb("mv_h", [128, G, 2])
        rec_sq = sb("rec_sq", [128, G])
        var_h = sb("var_h", [128, G])
        rstd_h = sb("rstd_h", [128, G])
        scale_h = sb("scale_h", [128, G])
        h_gain = sb("h_gain", [128, G, D])
        h_affine = sb("h_affine", [128, G, D])
        h_act = sb("h_act", [128, G, D])
        x1 = [sb(f"x1_{q}", [128, G, D]) for q in range(2)]
        st_f = sb("st_f", [128, G, 6])
        mv_f = sb("mv_f", [128, G, 2])
        var_f = sb("var_f", [128, G])
        rstd_f = sb("rstd_f", [128, G])
        y_norm = sb("y_norm", [128, G, D])
        xn = sb("xn", [128, T])
        xn_hi = [sb(f"xn_hi{q}", [128, T], F32R) for q in range(2)]
        xn_lo = [sb(f"xn_lo{q}", [128, T], F32R) for q in range(2)]
        logits = sb("logits", [128, G, E])
        top = sb("top", [128, G, 8])
        top_at = sb("top_at", [128, G, 8], U32)
        top_at_f = sb("top_at_f", [128, G, 2])
        top_gap = sb("top_gap", [128, G])
        top_exp = sb("top_exp", [128, G])
        top_den = sb("top_den", [128, G])
        top_w = sb("top_w", [128, G, 2])
        pick = sb("pick", [128, 2, G, E])
        picked = sb("picked", [128, 2, G, E])
        gate = [sb(f"gate{q}", [128, G, E]) for q in range(2)]
        gate_parts = sb("gate_parts", [128, 3, GE])
        gateT = sb("gateT", [3 * GE, 128], F32R)
        hid = [sb(f"hid{q}", [128, HH, T]) for q in range(NH)]
        acc = [sb(f"acc{q}", [128, G, D]) for q in range(2)]

        hid_bank = [bank(f"hid_bank{n}") for n in range(NHB)]
        y_bank = [bank(f"y_bank{n}") for n in range(NYB)]
        bank_b = bank("bank_b")
        pair = ctx.enter_context(nc.psum_tensor("pair", [128, 2, 512], F32))
        bank_a = pair[:, 0, :]
        Wh_cols = [pair[:, j // 2, (j % 2) * (D + 2):(j % 2 + 1) * (D + 2)] for j in range(G)]
        logit_cols = pair[:, 1, 2 * (D + 2):2 * (D + 2) + GE]
        gateT_cols = pair[0:3 * GE, 1, 384:512]

        w_loaded, gnn_loaded, ffn_loaded, experts_loaded = (
            sem(n + "_loaded") for n in "w gnn ffn experts".split())
        consts_ready, setup_pe = sem("consts_ready"), sem("setup_pe")
        ident_zero, b2_zero, b2_loaded = sem("ident_zero"), sem("b2_zero"), sem("b2_loaded")
        setup_act, w_split = sem("setup_act"), sem("w_split")
        x_loaded = [sem(f"x_loaded{q}") for q in range(2)]
        adj_loaded = [sem(f"adj_loaded{q}") for q in range(2)]
        stored = [sem(f"stored{q}") for q in range(2)]
        a_stats, a_aggr, a_eps, a_rstd, a_norm = (sem("a_" + n) for n in "stats aggr eps rstd norm".split())
        a_xT, a_xT_sb, a_score, a_Wh = (sem("a_" + n) for n in "xT xT_sb score Wh".split())
        a_lrelu, a_Wh_sb, a_mask, a_masked, a_max, a_prob = (
            sem("a_" + n) for n in "lrelu Wh_sb mask masked max prob".split())
        a_rec, a_probT, a_probT_sb = sem("a_rec"), sem("a_probT"), sem("a_probT_sb")
        r_h, r_sq, r_stats, r_aggr, r_var, r_eps, r_rstd, r_scale = (
            sem("r_" + n) for n in "h sq stats aggr var eps rstd scale".split())
        r_gain, r_affine, r_act, r_x1, f_stats, f_aggr, f_eps, f_rstd, f_norm = (
            sem("r_" + n) for n in "gain affine act x1 stats1 aggr1 eps1 rstd1 norm1".split())
        f_yT, f_xn, f_hi, f_lo, f_logits = (sem("f_" + n) for n in "yT xn hi lo logits".split())
        g_logits, g_top, g_at, g_at_f, g_gap, g_exp, g_den, g_w1, g_w2, g_pick, g_picked, g_gate, g_hi, g_parts = (
            sem("g_" + n) for n in "logits top at at_f gap exp den w1 w2 pick picked gate hi parts".split())
        g_T, g_T_sb = sem("g_T"), sem("g_T_sb")
        up = [sem(f"up{n}") for n in range(E * HH)]
        act = [sem(f"act{n}") for n in range(E * HH)]
        down = [sem(f"down{e}") for e in range(E)]
        added = [sem(f"added{e}") for e in range(E)]
        b_term, b_added = sem("b_term"), sem("b_added")

        uses = E * HH
        bank_before = []
        for n in range(uses):
            earlier = [m for m in range(n) if m % NHB == n % NHB]
            bank_before.append((earlier[-1], False) if earlier else
                               (max(m for m in range(uses) if m % NHB == n % NHB), True))

        block = ctx.enter_context(nc.Block())

        def run(eng, step, loads=False):
            def alone(k):
                step(Step(k, NB, lambda d: min(k + d, NB), lambda d: 16 * ((k + d) // 2 + 1)))

            for k in range(FIRST_STEP, LOOP_FROM):
                alone(k)
            with eng.Fori(0, (LOOP_TO - LOOP_FROM) // 2) as i:
                value = {d: eng.snap(eng.to_reg(2 * i + LOOP_FROM + d)) for d in range(-1, 6)}
                load = {d: eng.snap(eng.to_reg(16 * i + 16 * (LOOP_FROM // 2 + d))) for d in (0, 2, 3)} if loads else {}
                for u in range(2):
                    step(Step(LOOP_FROM + u, None, lambda d: value[u + d], lambda d: load[(u + d) // 2 + 1]))
            for k in range(LOOP_TO, LAST_STEP + 1):
                alone(k)

        @block.sync
        def _(sp):
            xv = x.rearrange("b t f -> t b f")
            av = adj.rearrange("b t f -> t b f")
            ov = out.rearrange("b t f -> t b f")

            def load(row, q):
                sp.dma_start(x_in[q][:, :, :], xv[:, row, :]).then_inc(x_loaded[q], 16)
                sp.dma_start(adj_in[q][:, :, :], av[:, row, :]).then_inc(adj_loaded[q], 16)

            load(slice(0, G), 0)
            sp.dma_start(W_ext[:, 0:D], gnn_W).then_inc(w_loaded, 16)
            for r in range(2):
                sp.dma_start(a_sb[:, r:r + 1], gnn_a[r * D:(r + 1) * D, :]).then_inc(w_loaded, 16)
            sp.dma_start(gnn_gamma_sb[:, :], gnn_gamma.partition_broadcast(128)).then_inc(gnn_loaded, 16)
            sp.dma_start(gnn_beta_sb[:, :], gnn_beta.partition_broadcast(128)).then_inc(gnn_loaded, 16)
            load(slice(G, 2 * G), 1)
            sp.dma_start(W1_sb[:, :, :], W1.rearrange("e k h -> k e h")).then_inc(experts_loaded, 16)
            sp.dma_start(W2_sb[:, :, :], W2.rearrange("e (a p) d -> p (e a) d", p=128)).then_inc(experts_loaded, 16)

            sp.dma_start(ffn_gamma_sb[:, :], ffn_gamma.unsqueeze(1)).then_inc(ffn_loaded, 16)
            sp.dma_start(ffn_beta_sb[:, :], ffn_beta.unsqueeze(1)).then_inc(ffn_loaded, 16)
            sp.dma_start(Wr_sb[:, :], Wr).then_inc(ffn_loaded, 16)
            sp.dma_start(br_sb[:, :], br.partition_broadcast(128)).then_inc(ffn_loaded, 16)
            sp.dma_start(b1_rows[:, :], b1.rearrange("e (a p) -> (e a) p", p=128)).then_inc(ffn_loaded, 16)
            sp.wait_ge(b2_zero, 1)
            for part in range(3):
                for j in range(G):
                    row = (part * G + j) * E
                    sp.dma_start(b2_blocks[row:row + E, j, :], b2).then_inc(b2_loaded, 16)

            def step(k, k_mod, count, blocks):
                if blocks or 0 <= k + 3 < NB and k + 3 >= 2:
                    sp.wait_ge(gnn_loaded, 16)
                    need(sp, r_x1, count(2))
                    need(sp, a_mask, count(2))
                    load(bass.ds((k + 3) * G, G), (k_mod + 3) % 2)
                if blocks or 0 <= k - 1 < NB:
                    sp.wait_ge(gnn_loaded, 16)
                    need(sp, added[E - 1], count(0))
                    sp.dma_start(ov[:, bass.ds((k - 1) * G, G), :], acc[(k_mod - 1) % 2][:, :, :]).then_inc(stored[(k_mod - 1) % 2], 16)

            for k in range(FIRST_STEP, LOOP_FROM):
                step(k, k, lambda d: k + d, False)
            with sp.Fori(0, (LOOP_TO - LOOP_FROM) // 2) as i:
                value = {d: sp.snap(sp.to_reg(2 * i + LOOP_FROM + d)) for d in range(0, 4)}
                for u in range(2):
                    step(2 * i + (LOOP_FROM + u), u, lambda d: value[u + d], True)
            for k in range(LOOP_TO, LAST_STEP + 1):
                step(k, k, lambda d: k + d, False)
            for q in range(2):
                sp.wait_ge(stored[q], 16 * (NB // 2))

        @block.gpsimd
        def _(pool):
            g = nc.gpsimd
            g.memset(ident[:, :], 0.0).then_inc(ident_zero, 1)
            g.memset(b2_blocks[:, :, :], 0.0).then_inc(b2_zero, 1)
            pool.wait_ge(ident_zero, 1)
            g.affine_select(out=ident[:, :], in_=ident[:, :], compare_op=ALU.not_equal, fill=1.0,
                            base=0, pattern=[[-1, 128]], channel_multiplier=1).then_inc(consts_ready, 1)
            g.memset(half_power[:, :], -0.5).then_inc(consts_ready, 1)
            g.memset(e_base[:, :], E_BASE).then_inc(consts_ready, 1)
            for e in range(E):
                g.memset(expert_ids[:, :, e:e + 1], float(e)).then_inc(consts_ready, 1)
            pool.wait_ge(consts_ready, 3 + E)

            def inverse_root(dst, done, started, value):
                need(pool, started, value)
                g.tensor_tensor(dst[:, :], dst[:, :], half_power[:, :], ALU.pow).then_inc(done, 1)

            def step(s):
                c = s.count
                for e in range(E):
                    if e == 0 and s.has(1):
                        need(pool, r_act, c(2))
                        need(pool, added[0], c(0))
                        g.tensor_tensor(x1[s.parity(1)][:, :, :], x_in[s.parity(1)][:, :, :], h_act[:, :, :],
                                        ALU.add).then_inc(r_x1, 1)
                    if e == 1 and s.has(1):
                        pool.wait_ge(consts_ready, 3)
                        need(pool, f_aggr, c(2))
                        need(pool, f_norm, c(1))
                        g.tensor_scalar(rstd_f[:, :], mv_f[:, :, 1], 1.0 + EPS, EPS * EPS,
                                        ALU.mult, ALU.add).then_inc(f_eps, 1)
                        inverse_root(rstd_f, f_rstd, f_eps, c(2))
                    if e == 4 and s.has(3):
                        pool.wait_ge(consts_ready, 3)
                        need(pool, a_aggr, c(4))
                        need(pool, a_norm, c(3))
                        g.tensor_scalar(rstd_a[:, :], mv_a[:, :, 1], EPS, 1.0, ALU.add, ALU.mult).then_inc(a_eps, 1)
                        inverse_root(rstd_a, a_rstd, a_eps, c(4))
                    if e == 4 and s.has(1):
                        need(pool, f_hi, c(2))
                        need(pool, up[uses - 1], c(0))
                        g.tensor_tensor(xn_lo[s.parity(1)][:, :], xn[:, :], xn_hi[s.parity(1)][:, :].bitcast(F32),
                                        ALU.subtract).then_inc(f_lo, 1)
                    if e == 5 and s.has(2):
                        need(pool, a_rec, c(3))
                        need(pool, r_var, c(2))
                        g.tensor_tensor(rec_sq[:, :], rec_sum[:, :], rec_sum[:, :], ALU.mult).then_inc(r_sq, 1)
                        need(pool, r_aggr, c(3))
                        need(pool, r_sq, c(3))
                        need(pool, r_eps, c(2))
                        g.tensor_tensor(var_h[:, :], mv_h[:, :, 1], rec_sq[:, :], ALU.mult).then_inc(r_var, 1)
                        pool.wait_ge(consts_ready, 3)
                        need(pool, r_var, c(3))
                        need(pool, r_scale, c(2))
                        g.tensor_scalar(rstd_h[:, :], var_h[:, :], EPS, 1.0, ALU.add, ALU.mult).then_inc(r_eps, 1)
                        inverse_root(rstd_h, r_rstd, r_eps, c(3))
                        need(pool, r_rstd, c(3))
                        need(pool, r_affine, c(2))
                        g.tensor_tensor(scale_h[:, :], rstd_h[:, :], rec_sum[:, :], ALU.mult).then_inc(r_scale, 1)
                    if e == 6 and s.has(1):
                        need(pool, g_gap, c(2))
                        need(pool, g_w2, c(1))
                        g.tensor_tensor(top_exp[:, :], e_base[:, :], top_gap[:, :], ALU.pow).then_inc(g_exp, 1)

            run(pool, step)

        @block.scalar
        def _(scalar):
            a = nc.scalar
            scalar.wait_ge(setup_pe, 1)
            a.copy(WT_sb[:, :], bank_a[:, 0:D]).then_inc(setup_act, 1)
            scalar.wait_ge(setup_pe, 2)
            a.copy(W_ext[:, D:D + 2], bank_b[:, 0:2]).then_inc(setup_act, 1)

            def gelu_expert(s, n):
                e, h = divmod(n, HH)
                need(scalar, up[n], s.count(1))
                need(scalar, down[(e - NH) % E], s.count(1 if e >= NH else 0))
                a.activation(hid[e % NH][:, h, :], hid_bank[n % NHB][:, :], ACT.Gelu,
                             bias=b1_sb[:, n:n + 1]).then_inc(act[n], 1)

            def graphs(ap):
                return ap[:, :].rearrange("p (g n) -> p g n", g=G)

            def step(s):
                c = s.count
                for e in range(E):
                    if e == 1 and s.has(2):
                        need(scalar, a_Wh, c(3))
                        need(scalar, r_h, c(2))
                        a.copy(Wh[:, :, :].rearrange("p (b g) n -> p b g n", b=2),
                               pair[:, :, 0:2 * (D + 2)].rearrange("p b (g n) -> p b g n", g=2)).then_inc(a_Wh_sb, 1)
                    if e == 3 and s.has(0):
                        need(scalar, g_T, c(1))
                        need(scalar, b_term, c(0))
                        a.copy(gateT[:, :], gateT_cols).then_inc(g_T_sb, 1)
                    if e == 4 and s.has(1):
                        need(scalar, f_yT, c(2))
                        need(scalar, f_logits, c(1))
                        need(scalar, f_lo, c(1))
                        a.activation(xn[:, :], bank_a[:, :], ACT.Identity, bias=ffn_beta_sb[:, :],
                                     scale=ffn_gamma_sb[:, :]).then_inc(f_xn, 1)
                        need(scalar, up[uses - 1], c(0))
                        a.activation(xn_hi[s.parity(1)][:, :], bank_a[:, :], ACT.Identity, bias=ffn_beta_sb[:, :],
                                     scale=ffn_gamma_sb[:, :]).then_inc(f_hi, 1)
                    if e == 4 and s.has(2):
                        need(scalar, a_probT, c(3))
                        need(scalar, r_h, c(2))
                        a.copy(probT[:, :, :], graphs(bank_b)).then_inc(a_probT_sb, 1)
                    if e == 5 and s.blocks is not None and s.k == -2:
                        scalar.wait_ge(setup_pe, 3)
                        a.copy(b1_sb[:, :], bank_a[:, 0:uses]).then_inc(setup_act, 1)
                    if e == 7 and s.has(2):
                        need(scalar, r_affine, c(3))
                        need(scalar, r_x1, c(2))
                        a.activation(h_act[:, :, :], h_affine[:, :, :], ACT.Gelu).then_inc(r_act, 1)
                    if s.has(0):
                        for h in range(HH):
                            gelu_expert(s, e * HH + h)
                    if e == 2 and s.has(2):
                        need(scalar, a_max, c(3))
                        need(scalar, a_probT, c(2))
                        need(scalar, a_rec, c(2))
                        for j in range(G):
                            ins = a.activation(prob[:, j, :], score[:, j, :], ACT.Exp, bias=neg_max[:, j:j + 1],
                                               accum_out=prob_sum[:, j:j + 1])
                        ins.then_inc(a_prob, 1)
                    if e == 7 and s.has(3):
                        need(scalar, a_xT, c(4))
                        need(scalar, a_score, c(3))
                        a.copy(x_normT[:, :], bank_a[:, :]).then_inc(a_xT_sb, 1)

            run(scalar, step)

        @block.vector
        def _(dve):
            v = nc.vector
            def split_W1_hi():
                dve.wait_ge(experts_loaded, 32)
                v.tensor_copy(W1_hi[:, :, :], W1_sb[:, :, :]).then_inc(w_split, 1)

            def split_W1_lo():
                dve.wait_ge(w_split, 1)
                v.tensor_tensor(W1_lo[:, :, :], W1_sb[:, :, :], W1_hi[:, :, :].bitcast(F32),
                                ALU.subtract).then_inc(w_split, 1)

            def split_b2():
                dve.wait_ge(b2_loaded, 16 * 3 * G)
                v.tensor_copy(b2_hi[:, :, :], b2_blocks[:, :, :]).then_inc(w_split, 1)
                v.tensor_copy(b2_parts[0:2 * GE, :, :], b2_blocks[0:2 * GE, :, :]).then_inc(w_split, 1)
                dve.wait_ge(w_split, 3)
                v.tensor_tensor(b2_parts[2 * GE:, :, :], b2_blocks[2 * GE:, :, :],
                                b2_hi[2 * GE:, :, :].bitcast(F32), ALU.subtract).then_inc(w_split, 1)

            def norm_stats(src, st, mv, stats_done, aggr_done, value):
                for j in range(G):
                    ins = v.bn_stats(st[:, j, :], src[j])
                ins.then_inc(stats_done, 1)
                dve.wait_ge(consts_ready, 1)
                need(dve, stats_done, value)
                for j in range(G):
                    ins = v.bn_aggr(mv[:, j, :], st[:, j, :])
                ins.then_inc(aggr_done, 1)

            def add_expert(e, q, value, s):
                if e == 0:
                    need(dve, g_gate, value)
                    need(dve, stored[q], s.loads(-2))
                else:
                    need(dve, added[e - 1], value)
                if e == BIAS_EXPERT:
                    need(dve, b_added, value)
                need(dve, down[e], value)
                before = x1[q] if e == 0 else acc[q]
                for j in range(G):
                    ins = v.scalar_tensor_tensor(acc[q][:, j, :], y_bank[e % NYB][:, j * D:(j + 1) * D],
                                                 gate[q][:, j, e:e + 1], before[:, j, :], ALU.mult, ALU.add)
                ins.then_inc(added[e], 1)

            def per_graph(ap):
                return [ap[:, j * D:(j + 1) * D] for j in range(G)]

            def normalise(dst, src, mv, rstd, done):
                for j in range(G):
                    ins = v.tensor_scalar(dst[:, j, :], src[j], mv[:, j, 0:1], rstd[:, j:j + 1],
                                          ALU.subtract, ALU.mult)
                ins.then_inc(done, 1)

            def graphs(ap):
                return [ap[:, j, :] for j in range(G)]

            def step(s):
                c = s.count
                for e in range(E):
                    if e == 0 and s.has(2):
                        need(dve, adj_loaded[s.parity(2)], s.loads(2))
                        need(dve, a_lrelu, c(2))
                        v.tensor_scalar(mask[:, :, :], adj_in[s.parity(2)][:, :, :], 0.0, NEG / LRELU_SLOPE,
                                        ALU.is_le, ALU.mult).then_inc(a_mask, 1)
                    if e == 1 and s.has(1):
                        need(dve, r_x1, c(2))
                        need(dve, f_rstd, c(1))
                        norm_stats(graphs(x1[s.parity(1)]), st_f, mv_f, f_stats, f_aggr, c(2))
                    if e < LAG and s.has(-1):
                        add_expert(E - LAG + e, s.parity(-1), c(0), s)
                    if e == 1 and s.has(2):
                        need(dve, a_score, c(3))
                        need(dve, a_mask, c(3))
                        need(dve, a_Wh_sb, c(3))
                        for j in range(G):
                            ins = v.scalar_tensor_tensor(mask[:, j, :], per_graph(bank_b)[j], Wh[:, j, D:D + 1],
                                                         mask[:, j, :], ALU.add, ALU.add)
                        ins.then_inc(a_masked, 1)
                        need(dve, a_masked, c(3))
                        need(dve, a_prob, c(2))
                        v.scalar_tensor_tensor(score[:, :, :], mask[:, :, :], LRELU_SLOPE, mask[:, :, :],
                                               ALU.mult, ALU.max).then_inc(a_lrelu, 1)
                        need(dve, a_lrelu, c(3))
                        v.tensor_reduce(neg_max[:, :], score[:, :, :], AX_X, ALU.max, negate=True).then_inc(a_max, 1)
                    if e == 2 and s.has(1):
                        need(dve, f_rstd, c(2))
                        need(dve, f_yT, c(1))
                        normalise(y_norm, graphs(x1[s.parity(1)]), mv_f, rstd_f, f_norm)
                    if e == 3 and s.blocks is not None and s.k == -2:
                        split_W1_hi()
                    if e == 3 and s.has(2):
                        need(dve, a_prob, c(3))
                        need(dve, r_scale, c(2))
                        v.reciprocal(rec_sum[:, :], prob_sum[:, :]).then_inc(a_rec, 1)
                    if e == 3 and s.has(3):
                        need(dve, x_loaded[s.parity(3)], s.loads(3))
                        need(dve, a_rstd, c(3))
                        norm_stats(graphs(x_in[s.parity(3)]), st_a, mv_a, a_stats, a_aggr, c(4))
                    if e == 5 and s.blocks is not None and s.k == -2:
                        split_W1_lo()
                    if e == 5 and s.blocks is not None and s.k == -1:
                        split_b2()
                    if e == 5 and s.has(3):
                        need(dve, a_rstd, c(4))
                        need(dve, a_xT, c(3))
                        normalise(x_norm, graphs(x_in[s.parity(3)]), mv_a, rstd_a, a_norm)
                    if e == 5 and s.has(2):
                        if s.blocks is not None and s.k == -2:
                            dve.wait_ge(gnn_loaded, 32)
                            dve.wait_ge(ffn_loaded, 16 * 5)
                        need(dve, r_h, c(3))
                        need(dve, r_var, c(2))
                        norm_stats(per_graph(bank_b), st_h, mv_h, r_stats, r_aggr, c(3))
                        need(dve, r_aggr, c(3))
                        need(dve, r_affine, c(2))
                        for j in range(G):
                            ins = v.scalar_tensor_tensor(h_gain[:, j, :], per_graph(bank_b)[j], mv_h[:, j, 0:1],
                                                         gnn_gamma_sb[:, :], ALU.subtract, ALU.mult)
                        ins.then_inc(r_gain, 1)
                    if e == 5 and s.has(1):
                        need(dve, f_logits, c(2))
                        v.tensor_tensor(logits[:, :, :],
                                        logit_cols.rearrange("p (g e) -> p g e", g=G),
                                        br_sb[:, :].unsqueeze(1).to_broadcast([128, G, E]),
                                        ALU.add).then_inc(g_logits, 1)
                        dve.wait_ge(consts_ready, 1)
                        need(dve, g_logits, c(2))
                        for j in range(G):
                            ins = v.max(top[:, j, :], logits[:, j, :])
                        ins.then_inc(g_top, 1)
                        dve.wait_ge(consts_ready, 1)
                        need(dve, g_top, c(2))
                        for j in range(G):
                            ins = v.max_index(top_at[:, j, :], top[:, j, :], logits[:, j, :])
                        ins.then_inc(g_at, 1)
                        v.tensor_tensor(top_gap[:, :], top[:, :, 1], top[:, :, 0], ALU.subtract).then_inc(g_gap, 1)
                        need(dve, g_at, c(2))
                        v.tensor_copy(top_at_f[:, :, :], top_at[:, :, 0:2]).then_inc(g_at_f, 1)
                        need(dve, g_at_f, c(2))
                        for r in range(2):
                            ins = v.tensor_tensor(pick[:, r, :, :], expert_ids[:, :, :],
                                                  top_at_f[:, :, r:r + 1].to_broadcast([128, G, E]), ALU.is_equal)
                        ins.then_inc(g_pick, 1)
                    if e == 6 and s.has(2):
                        need(dve, r_scale, c(3))
                        need(dve, r_gain, c(3))
                        need(dve, r_act, c(2))
                        for j in range(G):
                            ins = v.scalar_tensor_tensor(h_affine[:, j, :], h_gain[:, j, :], scale_h[:, j:j + 1],
                                                         gnn_beta_sb[:, :], ALU.mult, ALU.add)
                        ins.then_inc(r_affine, 1)
                    if e == 7 and s.has(1):
                        need(dve, g_exp, c(2))
                        v.tensor_scalar(top_den[:, :], top_exp[:, :], 1.0, None, ALU.add).then_inc(g_den, 1)
                        need(dve, g_den, c(2))
                        v.reciprocal(top_w[:, :, 0], top_den[:, :]).then_inc(g_w1, 1)
                        need(dve, g_w1, c(2))
                        v.tensor_tensor(top_w[:, :, 1], top_w[:, :, 0], top_exp[:, :], ALU.mult).then_inc(g_w2, 1)
                        need(dve, g_w2, c(2))
                        for r in range(2):
                            ins = v.tensor_tensor(picked[:, r, :, :], pick[:, r, :, :],
                                                  top_w[:, :, r:r + 1].to_broadcast([128, G, E]), ALU.mult)
                        ins.then_inc(g_picked, 1)
                        need(dve, g_picked, c(2))
                        need(dve, added[E - 1], c(0))
                        v.tensor_tensor(gate[s.parity(1)][:, :, :], picked[:, 0, :, :], picked[:, 1, :, :],
                                        ALU.add).then_inc(g_gate, 1)
                        need(dve, g_gate, c(2))
                        need(dve, g_T, c(1))
                        flat = gate[s.parity(1)][:, :, :].rearrange("p g e -> p (g e)")
                        v.tensor_copy(gate_parts[:, 0, :].bitcast(F32R), flat)
                        v.tensor_copy(gate_parts[:, 2, :].bitcast(F32R), flat).then_inc(g_hi, 1)
                        need(dve, g_hi, c(2))
                        v.tensor_tensor(gate_parts[:, 1, :], flat, gate_parts[:, 0, :],
                                        ALU.subtract).then_inc(g_parts, 1)
                    if e >= LAG and s.has(0):
                        if e - LAG == BIAS_EXPERT:
                            need(dve, b_term, c(1))
                            need(dve, added[BIAS_EXPERT - 1], c(1))
                            v.tensor_tensor(acc[s.parity(0)][:, :, :],
                                            bank_a.rearrange("p (g n) -> p g n", g=G),
                                            acc[s.parity(0)][:, :, :], ALU.add).then_inc(b_added, 1)
                        add_expert(e - LAG, s.parity(0), c(1), s)

            dve.wait_ge(consts_ready, 3 + E)
            run(dve, step, loads=True)

        @block.tensor
        def _(pe):
            t = nc.tensor
            pe.wait_ge(consts_ready, 1)
            pe.wait_ge(w_loaded, 48)
            t.transpose(bank_a[:, 0:D], W_ext[:, 0:D], ident[:, :]).then_inc(setup_pe, 1)
            pe.wait_ge(setup_act, 1)
            t.matmul(bank_b[:, 0:2], WT_sb[:, :], a_sb[:, :], start=True, stop=True).then_inc(setup_pe, 1)
            pe.wait_ge(setup_act, 2)

            def second_product(e, value, earlier):
                need(pe, act[e * HH + HH - 1], value)
                need(pe, added[(e - NYB) % E], value if e >= NYB else earlier)
                for j in range(G):
                    cols = slice(j * N, (j + 1) * N)
                    for h in range(HH):
                        ins = t.matmul(y_bank[e % NYB][:, j * D:(j + 1) * D], hid[e % NH][:, h, cols],
                                       W2_sb[:, e * HH + h, :], start=(h == 0), stop=(h == HH - 1))
                ins.then_inc(down[e], 1)

            def first_product(s, e):
                q = s.parity(0)
                for h in range(HH):
                    n = e * HH + h
                    before, wrapped = bank_before[n]
                    need(pe, act[before], s.count(0 if wrapped else 1))
                    cols = slice(h * 128, h * 128 + 128)
                    dst = hid_bank[n % NHB][:, :]
                    t.matmul(dst, W1_hi[:, e, cols], xn_lo[q][:, :], start=True, stop=False)
                    t.matmul(dst, W1_lo[:, e, cols], xn_hi[q][:, :], start=False, stop=False)
                    t.matmul(dst, W1_hi[:, e, cols], xn_hi[q][:, :], start=False, stop=True).then_inc(up[n], 1)

            def transposes(dst, src):
                for j in range(G):
                    ins = t.transpose(dst[:, j * 128:j * 128 + 128], src[j], ident[:, :])
                return ins

            def step(s):
                c = s.count
                if s.blocks is not None and s.k == 0:
                    pe.wait_ge(w_split, 5)
                for e in range(E):
                    if e < LAG and s.has(-1):
                        second_product(E - LAG + e, c(0), c(-1))
                    if e >= LAG and s.has(0):
                        second_product(e - LAG, c(1), c(0))
                    if s.has(0):
                        if e == 0:
                            need(pe, f_lo, c(1))
                        first_product(s, e)
                    if e == 0 and s.has(2):
                        need(pe, a_xT_sb, c(3))
                        need(pe, g_T_sb, c(0))
                        need(pe, g_logits, c(1))
                        for j in range(G):
                            ins = t.matmul(Wh_cols[j], x_normT[:, j * N:(j + 1) * N], W_ext[:, :],
                                           start=True, stop=True)
                        ins.then_inc(a_Wh, 1)
                    if e == 1 and s.has(2):
                        need(pe, a_Wh_sb, c(3))
                        need(pe, r_gain, c(2))
                        transposes(bank_b, [Wh[:, j, D + 1:D + 2].to_broadcast([128, 128]) for j in range(G)]).then_inc(
                            a_score, 1)
                    if e == 2 and s.has(0):
                        need(pe, g_parts, c(1))
                        need(pe, a_Wh_sb, c(3))
                        t.transpose(gateT_cols, gate_parts[:, :, :].rearrange("p s n -> p (s n)"),
                                    ident[:, :]).then_inc(g_T, 1)
                    if e == 3 and s.has(1):
                        need(pe, f_norm, c(2))
                        need(pe, a_Wh_sb, c(3))
                        transposes(bank_a, [y_norm[:, j, :] for j in range(G)]).then_inc(f_yT, 1)
                    if e == 3 and s.has(2):
                        need(pe, a_prob, c(3))
                        need(pe, a_masked, c(3))
                        transposes(bank_b, [prob[:, j, :] for j in range(G)]).then_inc(a_probT, 1)
                    if e == 4 and s.has(1):
                        need(pe, f_xn, c(2))
                        need(pe, g_T_sb, c(1))
                        for j in range(G):
                            ins = t.matmul(logit_cols[:, j * E:(j + 1) * E], xn[:, j * N:(j + 1) * N], Wr_sb[:, :],
                                           start=True, stop=True)
                        ins.then_inc(f_logits, 1)
                    if e == 4 and s.has(2):
                        need(pe, a_probT_sb, c(3))
                        need(pe, a_Wh_sb, c(3))
                        for j in range(G):
                            ins = t.matmul(bank_b[:, j * D:(j + 1) * D], probT[:, j, :], Wh[:, j, 0:D],
                                           start=True, stop=True)
                        ins.then_inc(r_h, 1)
                    if e == 4 and s.blocks is not None and s.k == -2:
                        pe.wait_ge(ffn_loaded, 16 * 5)
                        pe.wait_ge(a_Wh_sb, 1)
                        t.transpose(bank_a[:, 0:uses], b1_rows[:, :], ident[0:uses, 0:uses]).then_inc(setup_pe, 1)
                        pe.wait_ge(setup_act, 3)
                    if e == BIAS_SLOT and s.has(0):
                        need(pe, g_T_sb, c(1))
                        need(pe, f_hi, c(2))
                        t.matmul(bank_a[:, :], gateT[:, :], b2_parts[:, :, :].rearrange("p g d -> p (g d)"),
                                 start=True, stop=True).then_inc(b_term, 1)
                    if e == 7 and s.has(3):
                        need(pe, a_norm, c(4))
                        need(pe, b_added, c(1))
                        need(pe, f_hi, c(2))
                        transposes(bank_a, [x_norm[:, j, :] for j in range(G)]).then_inc(a_xT, 1)

            run(pe, step)


_INS = ["x", "adj", "L0_gnn_W", "L0_gnn_a", "L0_gnn_gamma", "L0_gnn_beta", "L0_ffn_gamma", "L0_ffn_beta",
        "L0_ffn_Wr", "L0_ffn_br", "L0_ffn_W1", "L0_ffn_b1", "L0_ffn_W2", "L0_ffn_b2"]


def kernel(**inputs):
    import numpy as np
    import concourse.bacc as bacc
    from concourse.bass_utils import run_bass_kernel_spmd

    nc = bacc.Bacc("TRN2", target_bir_lowering=False, num_devices=1)
    arrays, args = {}, []
    for name in _INS:
        arr = np.ascontiguousarray(inputs[name])
        arrays[name + "_dram"] = arr
        args.append(nc.dram_tensor(name + "_dram", arr.shape, mybir.dt.from_np(arr.dtype), kind="ExternalInput").ap())
    shape = inputs["x"].shape
    args.append(nc.dram_tensor("out_dram", shape, F32, kind="ExternalOutput").ap())
    gat_moe_kernel(nc, *args)
    r = run_bass_kernel_spmd(nc, [arrays], core_ids=[0])
    return r.results[0]["out_dram"]
```

```python
from contextlib import ExitStack

import concourse.bass as bass
from concourse import mybir

ALU = mybir.AluOpType
ACT = mybir.ActivationFunctionType
F32 = mybir.dt.float32
F32R = mybir.dt.float32r
U32 = mybir.dt.uint32
AX_X = mybir.AxisListType.X

LRELU_SLOPE = 0.2
EPS = 1e-5
NEG = -9e15
E_BASE = 2.718281828459045


class Step:

    def __init__(self, k, blocks, count, loads):
        self.k = k
        self.blocks = blocks
        self.count = count
        self.loads = loads

    def has(self, d):
        return self.blocks is None or 0 <= self.k + d < self.blocks

    def is_step(self, k):
        return self.blocks is not None and self.k == k

    def parity(self, d):
        return (self.k + d) % 2


def need(eng, sem, value):
    if isinstance(value, int) and value <= 0:
        return
    eng.wait_ge(sem, value)


def gat_moe_kernel(nc, x, adj, gnn_W, gnn_a, gnn_gamma, gnn_beta, ffn_gamma, ffn_beta,
                   Wr, br, W1, b1, W2, b2, out):
    B, N, D = x.shape
    E, _, H = W1.shape
    G = 4
    T = G * N
    NB = B // G
    HH = H // 128
    assert N == 128 and D == 128 and H == 256 and E == 8
    NHB, NYB = 3, 2
    LAG = 2
    NH = 4
    GE = G * E
    FIRST_STEP, LAST_STEP = -3, NB
    LOOP_FROM, LOOP_TO = 2, 2 + (NB - 5) // 2 * 2

    with ExitStack() as ctx:
        def sb(name, shape, dt=F32):
            return ctx.enter_context(nc.sbuf_tensor(name, shape, dt))

        def bank(name):
            return ctx.enter_context(nc.psum_tensor(name, [128, 512], F32))

        def sem(name):
            return ctx.enter_context(nc.semaphore(name))

        ident = sb("ident", [128, 128])
        expert_ids = sb("expert_ids", [128, G, E])
        half_power = sb("half_power", [128, G])
        e_base = sb("e_base", [128, G])
        W_sb = sb("W_sb", [128, D])
        WT_sb = sb("WT_sb", [128, D])
        a_sb = sb("a_sb", [128, 2])
        Wa = sb("Wa", [128, 2, D])
        gnn_gamma_sb = sb("gnn_gamma_sb", [128, D])
        gnn_beta_sb = sb("gnn_beta_sb", [128, D])
        ffn_gamma_sb = sb("ffn_gamma_sb", [128, 1])
        ffn_beta_sb = sb("ffn_beta_sb", [128, 1])
        Wr_sb = sb("Wr_sb", [128, E])
        br_sb = sb("br_sb", [128, E])
        W1_sb = sb("W1_sb", [128, E, H])
        W1_hi = sb("W1_hi", [128, E, H], F32R)
        W1_lo = sb("W1_lo", [128, E, H], F32R)
        W2_sb = sb("W2_sb", [128, E * HH, D])
        b1_rows = sb("b1_rows", [E * HH, 128])
        b1_sb = sb("b1_sb", [128, E * HH])
        b2_blocks = sb("b2_blocks", [3 * GE, G, D])
        b2_hi = sb("b2_hi", [3 * GE, G, D], F32R)
        b2_parts = sb("b2_parts", [3 * GE, G, D], F32R)

        x_in = [sb(f"x_in{q}", [128, G, D]) for q in range(2)]
        adj_in = [sb(f"adj_in{q}", [128, G, N]) for q in range(2)]
        st_a = sb("st_a", [128, G, 6])
        mv_a = sb("mv_a", [128, G, 2])
        rstd_a = sb("rstd_a", [128, G])
        x_norm = [sb(f"x_norm{q}", [128, G, D]) for q in range(2)]
        x_Wa = sb("x_Wa", [128, 2, G, D])
        s12 = sb("s12", [128, 2, G])
        score = sb("score", [128, G, N])
        mask = sb("mask", [128, G, N])
        neg_max = sb("neg_max", [128, G])
        prob = sb("prob", [128, G, N])
        prob_sum = sb("prob_sum", [128, G])
        rec_sum = sb("rec_sum", [128, G])
        probT = sb("probT", [128, G, N])
        mixT = sb("mixT", [128, G, N])
        st_h = sb("st_h", [128, G, 6])
        mv_h = sb("mv_h", [128, G, 2])
        rec_sq = sb("rec_sq", [128, G])
        var_h = sb("var_h", [128, G])
        rstd_h = sb("rstd_h", [128, G])
        scale_h = sb("scale_h", [128, G])
        h_gain = sb("h_gain", [128, G, D])
        h_affine = sb("h_affine", [128, G, D])
        h_act = sb("h_act", [128, G, D])
        x1 = [sb(f"x1_{q}", [128, G, D]) for q in range(2)]
        st_f = sb("st_f", [128, G, 6])
        mv_f = sb("mv_f", [128, G, 2])
        rstd_f = sb("rstd_f", [128, G])
        y_norm = sb("y_norm", [128, G, D])
        xn = sb("xn", [128, T])
        xn_hi = [sb(f"xn_hi{q}", [128, T], F32R) for q in range(2)]
        xn_lo = [sb(f"xn_lo{q}", [128, T], F32R) for q in range(2)]
        logits = sb("logits", [128, G, E])
        top = sb("top", [128, G, 8])
        top_at = sb("top_at", [128, G, 8], U32)
        top_at_f = sb("top_at_f", [128, G, 2])
        top_gap = sb("top_gap", [128, G])
        top_exp = sb("top_exp", [128, G])
        top_den = sb("top_den", [128, G])
        top_w = sb("top_w", [128, G, 2])
        pick = sb("pick", [128, 2, G, E])
        picked = sb("picked", [128, 2, G, E])
        gate = [sb(f"gate{q}", [128, G, E]) for q in range(2)]
        gate_parts = sb("gate_parts", [128, 3, GE])
        gateT = sb("gateT", [3 * GE, 128], F32R)
        hid = [sb(f"hid{q}", [128, HH, T]) for q in range(NH)]
        acc = [sb(f"acc{q}", [128, G, D]) for q in range(2)]

        hid_bank = [bank(f"hid_bank{n}") for n in range(NHB)]
        y_bank = [bank(f"y_bank{n}") for n in range(NYB)]
        bank_a = bank("bank_a")
        bank_b = bank("bank_b")
        bank_c = bank("bank_c")

        w_loaded, gnn_loaded, ffn_loaded, experts_loaded = (
            sem(n + "_loaded") for n in "w gnn ffn experts".split())
        consts_ready, setup_pe = sem("consts_ready"), sem("setup_pe")
        ident_zero, b2_zero, b2_loaded = sem("ident_zero"), sem("b2_zero"), sem("b2_loaded")
        setup_act, w_split = sem("setup_act"), sem("w_split")
        x_loaded = [sem(f"x_loaded{q}") for q in range(2)]
        adj_loaded = [sem(f"adj_loaded{q}") for q in range(2)]
        stored = [sem(f"stored{q}") for q in range(2)]
        a_stats, a_aggr, a_eps, a_rstd, a_norm = (sem("a_" + n) for n in "stats aggr eps rstd norm".split())
        a_prod, a_s12, a_score, a_mix, a_mix_sb = (sem("a_" + n) for n in "prod s12 score mix mix_sb".split())
        a_lrelu, a_mask, a_masked, a_max, a_prob = (
            sem("a_" + n) for n in "lrelu mask masked max prob".split())
        a_rec, a_probT, a_probT_sb = sem("a_rec"), sem("a_probT"), sem("a_probT_sb")
        r_h, r_sq, r_stats, r_aggr, r_var, r_eps, r_rstd, r_scale = (
            sem("r_" + n) for n in "h sq stats aggr var eps rstd scale".split())
        r_gain, r_affine, r_act, r_x1 = (sem("r_" + n) for n in "gain affine act x1".split())
        f_stats, f_aggr, f_eps, f_rstd, f_norm = (sem("f_" + n) for n in "stats aggr eps rstd norm".split())
        f_yT, f_xn, f_hi, f_lo, f_logits = (sem("f_" + n) for n in "yT xn hi lo logits".split())
        g_logits, g_top, g_at, g_at_f, g_gap, g_exp, g_den, g_w1, g_w2, g_pick, g_picked, g_gate, g_hi, g_parts = (
            sem("g_" + n) for n in "logits top at at_f gap exp den w1 w2 pick picked gate hi parts".split())
        g_T, g_T_sb = sem("g_T"), sem("g_T_sb")
        up = [sem(f"up{n}") for n in range(E * HH)]
        act = [sem(f"act{n}") for n in range(E * HH)]
        down = [sem(f"down{e}") for e in range(E)]
        added = [sem(f"added{e}") for e in range(E)]
        b_term, b_added = sem("b_term"), sem("b_added")

        uses = E * HH
        bank_before = []
        for n in range(uses):
            earlier = [m for m in range(n) if m % NHB == n % NHB]
            bank_before.append((earlier[-1], False) if earlier else
                               (max(m for m in range(uses) if m % NHB == n % NHB), True))

        block = ctx.enter_context(nc.Block())

        def run(eng, step, loads=False):
            def alone(k):
                step(Step(k, NB, lambda d: min(k + d, NB), lambda d: 16 * ((k + d) // 2 + 1)))

            for k in range(FIRST_STEP, LOOP_FROM):
                alone(k)
            with eng.Fori(0, (LOOP_TO - LOOP_FROM) // 2) as i:
                value = {d: eng.snap(eng.to_reg(2 * i + LOOP_FROM + d)) for d in range(-1, 6)}
                load = {d: eng.snap(eng.to_reg(16 * i + 16 * (LOOP_FROM // 2 + d))) for d in (0, 2, 3)} if loads else {}
                for u in range(2):
                    step(Step(LOOP_FROM + u, None, lambda d: value[u + d], lambda d: load[(u + d) // 2 + 1]))
            for k in range(LOOP_TO, LAST_STEP + 1):
                alone(k)

        @block.sync
        def _(sp):
            xv = x.rearrange("b t f -> t b f")
            av = adj.rearrange("b t f -> t b f")
            ov = out.rearrange("b t f -> t b f")

            def load(row, q):
                sp.dma_start(x_in[q][:, :, :], xv[:, row, :]).then_inc(x_loaded[q], 16)
                sp.dma_start(adj_in[q][:, :, :], av[:, row, :]).then_inc(adj_loaded[q], 16)

            load(slice(0, G), 0)
            sp.dma_start(W_sb[:, :], gnn_W).then_inc(w_loaded, 16)
            for r in range(2):
                sp.dma_start(a_sb[:, r:r + 1], gnn_a[r * D:(r + 1) * D, :]).then_inc(w_loaded, 16)
            sp.dma_start(gnn_gamma_sb[:, :], gnn_gamma.partition_broadcast(128)).then_inc(gnn_loaded, 16)
            sp.dma_start(gnn_beta_sb[:, :], gnn_beta.partition_broadcast(128)).then_inc(gnn_loaded, 16)
            load(slice(G, 2 * G), 1)
            sp.dma_start(W1_sb[:, :, :], W1.rearrange("e k h -> k e h")).then_inc(experts_loaded, 16)
            sp.dma_start(W2_sb[:, :, :], W2.rearrange("e (a p) d -> p (e a) d", p=128)).then_inc(experts_loaded, 16)

            sp.dma_start(ffn_gamma_sb[:, :], ffn_gamma.unsqueeze(1)).then_inc(ffn_loaded, 16)
            sp.dma_start(ffn_beta_sb[:, :], ffn_beta.unsqueeze(1)).then_inc(ffn_loaded, 16)
            sp.dma_start(Wr_sb[:, :], Wr).then_inc(ffn_loaded, 16)
            sp.dma_start(br_sb[:, :], br.partition_broadcast(128)).then_inc(ffn_loaded, 16)
            sp.dma_start(b1_rows[:, :], b1.rearrange("e (a p) -> (e a) p", p=128)).then_inc(ffn_loaded, 16)
            sp.wait_ge(b2_zero, 1)
            for part in range(3):
                for j in range(G):
                    row = (part * G + j) * E
                    sp.dma_start(b2_blocks[row:row + E, j, :], b2).then_inc(b2_loaded, 16)

            def step(k, k_mod, count, blocks):
                if blocks or 0 <= k + 3 < NB and k + 3 >= 2:
                    sp.wait_ge(w_loaded, 48)
                    need(sp, r_x1, count(2))
                    need(sp, a_mask, count(2))
                    load(bass.ds((k + 3) * G, G), (k_mod + 3) % 2)
                if blocks or 0 <= k - 1 < NB:
                    sp.wait_ge(w_loaded, 48)
                    need(sp, added[E - 1], count(0))
                    q = (k_mod - 1) % 2
                    sp.dma_start(ov[:, bass.ds((k - 1) * G, G), :], acc[q][:, :, :]).then_inc(stored[q], 16)

            for k in range(FIRST_STEP, LOOP_FROM):
                step(k, k, lambda d: k + d, False)
            with sp.Fori(0, (LOOP_TO - LOOP_FROM) // 2) as i:
                value = {d: sp.snap(sp.to_reg(2 * i + LOOP_FROM + d)) for d in range(0, 4)}
                for u in range(2):
                    step(2 * i + (LOOP_FROM + u), u, lambda d: value[u + d], True)
            for k in range(LOOP_TO, LAST_STEP + 1):
                step(k, k, lambda d: k + d, False)
            for q in range(2):
                sp.wait_ge(stored[q], 16 * (NB // 2))

        @block.gpsimd
        def _(pool):
            g = nc.gpsimd
            g.memset(ident[:, :], 0.0).then_inc(ident_zero, 1)
            g.memset(b2_blocks[:, :, :], 0.0).then_inc(b2_zero, 1)
            pool.wait_ge(ident_zero, 1)
            g.affine_select(out=ident[:, :], in_=ident[:, :], compare_op=ALU.not_equal, fill=1.0,
                            base=0, pattern=[[-1, 128]], channel_multiplier=1).then_inc(consts_ready, 1)
            g.memset(half_power[:, :], -0.5).then_inc(consts_ready, 1)
            g.memset(e_base[:, :], E_BASE).then_inc(consts_ready, 1)
            for e in range(E):
                g.memset(expert_ids[:, :, e:e + 1], float(e)).then_inc(consts_ready, 1)
            pool.wait_ge(consts_ready, 3 + E)

            def inverse_root(dst, done, started, value):
                need(pool, started, value)
                g.tensor_tensor(dst[:, :], dst[:, :], half_power[:, :], ALU.pow).then_inc(done, 1)

            def step(s):
                c = s.count
                for e in range(E):
                    if e == 0 and s.has(1):
                        need(pool, r_act, c(2))
                        need(pool, b_added, c(0))
                        g.tensor_tensor(x1[s.parity(1)][:, :, :], x_in[s.parity(1)][:, :, :], h_act[:, :, :],
                                        ALU.add).then_inc(r_x1, 1)
                    if e == 2 and s.has(1):
                        pool.wait_ge(consts_ready, 3)
                        need(pool, f_aggr, c(2))
                        need(pool, f_norm, c(1))
                        g.tensor_scalar(rstd_f[:, :], mv_f[:, :, 1], 1.0 + EPS, EPS * EPS,
                                        ALU.mult, ALU.add).then_inc(f_eps, 1)
                        inverse_root(rstd_f, f_rstd, f_eps, c(2))
                    if e == 4 and s.has(3):
                        pool.wait_ge(consts_ready, 3)
                        need(pool, a_aggr, c(4))
                        need(pool, a_norm, c(3))
                        g.tensor_scalar(rstd_a[:, :], mv_a[:, :, 1], EPS, 1.0, ALU.add, ALU.mult).then_inc(a_eps, 1)
                        inverse_root(rstd_a, a_rstd, a_eps, c(4))
                    if e == 4 and s.is_step(FIRST_STEP):
                        pool.wait_ge(setup_act, 2)
                    if e == 4 and s.has(3):
                        need(pool, a_norm, c(4))
                        need(pool, a_s12, c(3))
                        for r in range(2):
                            ins = g.tensor_tensor(x_Wa[:, r, :, :], x_norm[s.parity(3)][:, :, :],
                                                  Wa[:, r:r + 1, :].to_broadcast([128, G, D]), ALU.mult)
                        ins.then_inc(a_prod, 1)
                    if e == 5 and s.has(1):
                        need(pool, f_hi, c(2))
                        need(pool, up[uses - 1], c(0))
                        g.tensor_tensor(xn_lo[s.parity(1)][:, :], xn[:, :], xn_hi[s.parity(1)][:, :].bitcast(F32),
                                        ALU.subtract).then_inc(f_lo, 1)
                    if e == 5 and s.has(2):
                        need(pool, a_rec, c(3))
                        need(pool, r_var, c(2))
                        g.tensor_tensor(rec_sq[:, :], rec_sum[:, :], rec_sum[:, :], ALU.mult).then_inc(r_sq, 1)
                        need(pool, r_aggr, c(3))
                        need(pool, r_sq, c(3))
                        need(pool, r_eps, c(2))
                        g.tensor_tensor(var_h[:, :], mv_h[:, :, 1], rec_sq[:, :], ALU.mult).then_inc(r_var, 1)
                        pool.wait_ge(consts_ready, 3)
                        need(pool, r_var, c(3))
                        need(pool, r_scale, c(2))
                        g.tensor_scalar(rstd_h[:, :], var_h[:, :], EPS, 1.0, ALU.add, ALU.mult).then_inc(r_eps, 1)
                        inverse_root(rstd_h, r_rstd, r_eps, c(3))
                        need(pool, r_rstd, c(3))
                        need(pool, r_affine, c(2))
                        g.tensor_tensor(scale_h[:, :], rstd_h[:, :], rec_sum[:, :], ALU.mult).then_inc(r_scale, 1)
                    if e == 6 and s.has(1):
                        need(pool, g_gap, c(2))
                        need(pool, g_w2, c(1))
                        g.tensor_tensor(top_exp[:, :], e_base[:, :], top_gap[:, :], ALU.pow).then_inc(g_exp, 1)

            run(pool, step)

        @block.scalar
        def _(scalar):
            a = nc.scalar
            scalar.wait_ge(setup_pe, 1)
            a.copy(WT_sb[:, :], bank_a[:, 0:D]).then_inc(setup_act, 1)
            scalar.wait_ge(setup_pe, 2)
            a.copy(Wa[:, :, :], bank_b[:, 0:2 * D].rearrange("p (r d) -> p r d", r=2)).then_inc(setup_act, 1)

            def gelu_expert(s, n):
                e, h = divmod(n, HH)
                need(scalar, up[n], s.count(1))
                need(scalar, down[(e - NH) % E], s.count(1 if e >= NH else 0))
                a.activation(hid[e % NH][:, h, :], hid_bank[n % NHB][:, :], ACT.Gelu,
                             bias=b1_sb[:, n:n + 1]).then_inc(act[n], 1)

            def graphs(ap):
                return ap[:, :].rearrange("p (g n) -> p g n", g=G)

            def step(s):
                c = s.count
                for e in range(E):
                    if e == 1 and s.has(0):
                        need(scalar, g_T, c(1))
                        need(scalar, b_term, c(0))
                        a.copy(gateT[:, :], bank_c[0:3 * GE, 0:128]).then_inc(g_T_sb, 1)
                    if e == 4 and s.has(2):
                        need(scalar, a_probT, c(3))
                        need(scalar, a_mix, c(2))
                        need(scalar, r_h, c(2))
                        a.copy(probT[:, :, :], graphs(bank_b)).then_inc(a_probT_sb, 1)
                    if e == 5 and s.has(2):
                        need(scalar, a_mix, c(3))
                        need(scalar, r_h, c(2))
                        a.copy(mixT[:, :, :], graphs(bank_c)).then_inc(a_mix_sb, 1)
                    if e == 5 and s.has(1):
                        need(scalar, f_yT, c(2))
                        need(scalar, f_logits, c(1))
                        need(scalar, f_lo, c(1))
                        a.activation(xn[:, :], bank_a[:, :], ACT.Identity, bias=ffn_beta_sb[:, :],
                                     scale=ffn_gamma_sb[:, :]).then_inc(f_xn, 1)
                        need(scalar, up[uses - 1], c(0))
                        a.activation(xn_hi[s.parity(1)][:, :], bank_a[:, :], ACT.Identity, bias=ffn_beta_sb[:, :],
                                     scale=ffn_gamma_sb[:, :]).then_inc(f_hi, 1)
                    if e == 5 and s.is_step(-2):
                        scalar.wait_ge(setup_pe, 3)
                        a.copy(b1_sb[:, :], bank_a[:, 0:uses]).then_inc(setup_act, 1)
                    if s.has(0):
                        for h in range(HH):
                            gelu_expert(s, e * HH + h)
                    if e == 1 and s.has(2):
                        need(scalar, a_max, c(3))
                        need(scalar, a_probT, c(2))
                        need(scalar, a_rec, c(2))
                        for j in range(G):
                            ins = a.activation(prob[:, j, :], score[:, j, :], ACT.Exp, bias=neg_max[:, j:j + 1],
                                               accum_out=prob_sum[:, j:j + 1])
                        ins.then_inc(a_prob, 1)
                    if e == 7 and s.has(2):
                        need(scalar, r_affine, c(3))
                        need(scalar, r_x1, c(2))
                        a.activation(h_act[:, :, :], h_affine[:, :, :], ACT.Gelu).then_inc(r_act, 1)

            run(scalar, step)

        @block.vector
        def _(dve):
            v = nc.vector

            def split_W1_hi():
                dve.wait_ge(experts_loaded, 32)
                v.tensor_copy(W1_hi[:, :, :], W1_sb[:, :, :]).then_inc(w_split, 1)

            def split_W1_lo():
                dve.wait_ge(w_split, 1)
                v.tensor_tensor(W1_lo[:, :, :], W1_sb[:, :, :], W1_hi[:, :, :].bitcast(F32),
                                ALU.subtract).then_inc(w_split, 1)

            def split_b2():
                dve.wait_ge(b2_loaded, 16 * 3 * G)
                v.tensor_copy(b2_hi[:, :, :], b2_blocks[:, :, :]).then_inc(w_split, 1)
                v.tensor_copy(b2_parts[0:2 * GE, :, :], b2_blocks[0:2 * GE, :, :]).then_inc(w_split, 1)
                dve.wait_ge(w_split, 3)
                v.tensor_tensor(b2_parts[2 * GE:, :, :], b2_blocks[2 * GE:, :, :],
                                b2_hi[2 * GE:, :, :].bitcast(F32), ALU.subtract).then_inc(w_split, 1)

            def norm_stats(src, st, mv, stats_done, aggr_done, value):
                for j in range(G):
                    ins = v.bn_stats(st[:, j, :], src[j])
                ins.then_inc(stats_done, 1)
                dve.wait_ge(consts_ready, 1)
                need(dve, stats_done, value)
                for j in range(G):
                    ins = v.bn_aggr(mv[:, j, :], st[:, j, :])
                ins.then_inc(aggr_done, 1)

            def add_expert(e, q, value):
                need(dve, added[e - 1] if e else b_added, value)
                need(dve, g_gate, value)
                need(dve, down[e], value)
                for j in range(G):
                    ins = v.scalar_tensor_tensor(acc[q][:, j, :], y_bank[e % NYB][:, j * D:(j + 1) * D],
                                                 gate[q][:, j, e:e + 1], acc[q][:, j, :], ALU.mult, ALU.add)
                ins.then_inc(added[e], 1)

            def per_graph(ap):
                return [ap[:, j * D:(j + 1) * D] for j in range(G)]

            def normalise(dst, src, mv, rstd, done):
                for j in range(G):
                    ins = v.tensor_scalar(dst[:, j, :], src[j], mv[:, j, 0:1], rstd[:, j:j + 1],
                                          ALU.subtract, ALU.mult)
                ins.then_inc(done, 1)

            def graphs(ap):
                return [ap[:, j, :] for j in range(G)]

            def step(s):
                c = s.count
                for e in range(E):
                    if e == 0 and s.has(2):
                        need(dve, adj_loaded[s.parity(2)], s.loads(2))
                        need(dve, a_lrelu, c(2))
                        v.tensor_scalar(mask[:, :, :], adj_in[s.parity(2)][:, :, :], 0.0, NEG / LRELU_SLOPE,
                                        ALU.is_le, ALU.mult).then_inc(a_mask, 1)
                    if e < LAG and s.has(-1):
                        add_expert(E - LAG + e, s.parity(-1), c(0))
                    if e == 0 and s.has(2):
                        need(dve, a_score, c(3))
                        need(dve, a_mask, c(3))
                        need(dve, a_s12, c(3))
                        for j in range(G):
                            ins = v.scalar_tensor_tensor(mask[:, j, :], per_graph(bank_b)[j], s12[:, 0, j:j + 1],
                                                         mask[:, j, :], ALU.add, ALU.add)
                        ins.then_inc(a_masked, 1)
                        need(dve, a_masked, c(3))
                        need(dve, a_prob, c(2))
                        v.scalar_tensor_tensor(score[:, :, :], mask[:, :, :], LRELU_SLOPE, mask[:, :, :],
                                               ALU.mult, ALU.max).then_inc(a_lrelu, 1)
                        need(dve, a_lrelu, c(3))
                        v.tensor_reduce(neg_max[:, :], score[:, :, :], AX_X, ALU.max, negate=True).then_inc(a_max, 1)
                    if e == 2 and s.has(1):
                        need(dve, r_x1, c(2))
                        need(dve, f_rstd, c(1))
                        norm_stats(graphs(x1[s.parity(1)]), st_f, mv_f, f_stats, f_aggr, c(2))
                    if e == 3 and s.has(2):
                        need(dve, a_prob, c(3))
                        need(dve, r_scale, c(2))
                        v.reciprocal(rec_sum[:, :], prob_sum[:, :]).then_inc(a_rec, 1)
                    if e == 5 and s.is_step(-2):
                        split_W1_lo()
                    if e == 5 and s.is_step(-1):
                        split_b2()
                    if e == 3 and s.has(1):
                        need(dve, f_rstd, c(2))
                        need(dve, f_yT, c(1))
                        normalise(y_norm, graphs(x1[s.parity(1)]), mv_f, rstd_f, f_norm)
                    if e == 3 and s.has(3):
                        need(dve, x_loaded[s.parity(3)], s.loads(3))
                        need(dve, a_rstd, c(3))
                        norm_stats(graphs(x_in[s.parity(3)]), st_a, mv_a, a_stats, a_aggr, c(4))
                    if e == 3 and s.is_step(-2):
                        split_W1_hi()
                    if e == 4 and s.has(3):
                        need(dve, a_rstd, c(4))
                        need(dve, a_mix, c(2))
                        normalise(x_norm[s.parity(3)], graphs(x_in[s.parity(3)]), mv_a, rstd_a, a_norm)
                    if e == 6 and s.has(2):
                        if s.is_step(-2):
                            dve.wait_ge(gnn_loaded, 32)
                            dve.wait_ge(ffn_loaded, 16 * 5)
                        need(dve, r_h, c(3))
                        need(dve, r_var, c(2))
                        norm_stats(per_graph(bank_b), st_h, mv_h, r_stats, r_aggr, c(3))
                        need(dve, r_aggr, c(3))
                        need(dve, r_affine, c(2))
                        for j in range(G):
                            ins = v.scalar_tensor_tensor(h_gain[:, j, :], per_graph(bank_b)[j], mv_h[:, j, 0:1],
                                                         gnn_gamma_sb[:, :], ALU.subtract, ALU.mult)
                        ins.then_inc(r_gain, 1)
                    if e == 6 and s.has(3):
                        need(dve, a_prod, c(4))
                        need(dve, a_masked, c(3))
                        need(dve, a_score, c(3))
                        v.tensor_reduce(s12[:, :, :], x_Wa[:, :, :, :], AX_X, ALU.add).then_inc(a_s12, 1)
                    if e == 6 and s.has(1):
                        need(dve, f_logits, c(2))
                        v.tensor_tensor(logits[:, :, :],
                                        bank_a[:, 0:GE].rearrange("p (g e) -> p g e", g=G),
                                        br_sb[:, :].unsqueeze(1).to_broadcast([128, G, E]),
                                        ALU.add).then_inc(g_logits, 1)
                        dve.wait_ge(consts_ready, 1)
                        need(dve, g_logits, c(2))
                        for j in range(G):
                            ins = v.max(top[:, j, :], logits[:, j, :])
                        ins.then_inc(g_top, 1)
                        dve.wait_ge(consts_ready, 1)
                        need(dve, g_top, c(2))
                        for j in range(G):
                            ins = v.max_index(top_at[:, j, :], top[:, j, :], logits[:, j, :])
                        ins.then_inc(g_at, 1)
                        v.tensor_tensor(top_gap[:, :], top[:, :, 1], top[:, :, 0], ALU.subtract).then_inc(g_gap, 1)
                        need(dve, g_at, c(2))
                        v.tensor_copy(top_at_f[:, :, :], top_at[:, :, 0:2]).then_inc(g_at_f, 1)
                        need(dve, g_at_f, c(2))
                        for r in range(2):
                            ins = v.tensor_tensor(pick[:, r, :, :], expert_ids[:, :, :],
                                                  top_at_f[:, :, r:r + 1].to_broadcast([128, G, E]), ALU.is_equal)
                        ins.then_inc(g_pick, 1)
                    if e == 7 and s.has(2):
                        need(dve, r_scale, c(3))
                        need(dve, r_gain, c(3))
                        need(dve, r_act, c(2))
                        for j in range(G):
                            ins = v.scalar_tensor_tensor(h_affine[:, j, :], h_gain[:, j, :], scale_h[:, j:j + 1],
                                                         gnn_beta_sb[:, :], ALU.mult, ALU.add)
                        ins.then_inc(r_affine, 1)
                    if e == 7 and s.has(1):
                        need(dve, g_exp, c(2))
                        v.tensor_scalar(top_den[:, :], top_exp[:, :], 1.0, None, ALU.add).then_inc(g_den, 1)
                        need(dve, g_den, c(2))
                        v.reciprocal(top_w[:, :, 0], top_den[:, :]).then_inc(g_w1, 1)
                        need(dve, g_w1, c(2))
                        v.tensor_tensor(top_w[:, :, 1], top_w[:, :, 0], top_exp[:, :], ALU.mult).then_inc(g_w2, 1)
                        need(dve, g_w2, c(2))
                        for r in range(2):
                            ins = v.tensor_tensor(picked[:, r, :, :], pick[:, r, :, :],
                                                  top_w[:, :, r:r + 1].to_broadcast([128, G, E]), ALU.mult)
                        ins.then_inc(g_picked, 1)
                        need(dve, g_picked, c(2))
                        need(dve, added[E - 1], c(0))
                        v.tensor_tensor(gate[s.parity(1)][:, :, :], picked[:, 0, :, :], picked[:, 1, :, :],
                                        ALU.add).then_inc(g_gate, 1)
                        need(dve, g_gate, c(2))
                        need(dve, g_T, c(1))
                        flat = gate[s.parity(1)][:, :, :].rearrange("p g e -> p (g e)")
                        v.tensor_copy(gate_parts[:, 0, :].bitcast(F32R), flat)
                        v.tensor_copy(gate_parts[:, 2, :].bitcast(F32R), flat).then_inc(g_hi, 1)
                        need(dve, g_hi, c(2))
                        v.tensor_tensor(gate_parts[:, 1, :], flat, gate_parts[:, 0, :],
                                        ALU.subtract).then_inc(g_parts, 1)
                    if e >= LAG and s.has(0):
                        if e == LAG:
                            need(dve, b_term, c(1))
                            need(dve, stored[s.parity(0)], s.loads(-2))
                            v.tensor_tensor(acc[s.parity(0)][:, :, :],
                                            bank_a[:, :].rearrange("p (g n) -> p g n", g=G),
                                            x1[s.parity(0)][:, :, :], ALU.add).then_inc(b_added, 1)
                        add_expert(e - LAG, s.parity(0), c(1))

            dve.wait_ge(consts_ready, 3 + E)
            run(dve, step, loads=True)

        @block.tensor
        def _(pe):
            t = nc.tensor
            pe.wait_ge(consts_ready, 1)
            pe.wait_ge(w_loaded, 48)
            t.transpose(bank_a[:, 0:D], W_sb[:, :], ident[:, :]).then_inc(setup_pe, 1)
            pe.wait_ge(setup_act, 1)
            for r in range(2):
                ins = t.matmul(bank_b[:, r * D:(r + 1) * D], a_sb[:, r:r + 1].to_broadcast([128, 128]), WT_sb[:, :],
                               start=True, stop=True)
            ins.then_inc(setup_pe, 1)
            pe.wait_ge(setup_act, 2)

            def second_product(e, value, earlier):
                need(pe, act[e * HH + HH - 1], value)
                need(pe, added[(e - NYB) % E], value if e >= NYB else earlier)
                for j in range(G):
                    cols = slice(j * N, (j + 1) * N)
                    for h in range(HH):
                        ins = t.matmul(y_bank[e % NYB][:, j * D:(j + 1) * D], hid[e % NH][:, h, cols],
                                       W2_sb[:, e * HH + h, :], start=(h == 0), stop=(h == HH - 1))
                ins.then_inc(down[e], 1)

            def first_product(s, e):
                q = s.parity(0)
                for h in range(HH):
                    n = e * HH + h
                    before, wrapped = bank_before[n]
                    need(pe, act[before], s.count(0 if wrapped else 1))
                    cols = slice(h * 128, h * 128 + 128)
                    dst = hid_bank[n % NHB][:, :]
                    t.matmul(dst, W1_hi[:, e, cols], xn_lo[q][:, :], start=True, stop=False)
                    t.matmul(dst, W1_lo[:, e, cols], xn_hi[q][:, :], start=False, stop=False)
                    t.matmul(dst, W1_hi[:, e, cols], xn_hi[q][:, :], start=False, stop=True).then_inc(up[n], 1)

            def transposes(dst, src):
                for j in range(G):
                    ins = t.transpose(dst[:, j * 128:j * 128 + 128], src[j], ident[:, :])
                return ins

            def step(s):
                c = s.count
                if s.is_step(0):
                    pe.wait_ge(w_split, 2)
                for e in range(E):
                    if e < LAG and s.has(-1):
                        second_product(E - LAG + e, c(0), c(-1))
                    if e >= LAG and s.has(0):
                        second_product(e - LAG, c(1), c(0))
                    if s.has(0):
                        if e == 0:
                            need(pe, f_lo, c(1))
                        first_product(s, e)
                    if e == 0 and s.has(2):
                        need(pe, a_s12, c(3))
                        need(pe, r_gain, c(2))
                        transposes(bank_b, [s12[:, 1, j:j + 1].to_broadcast([128, 128]) for j in range(G)]).then_inc(
                            a_score, 1)
                    if e == 0 and s.has(0):
                        need(pe, g_parts, c(1))
                        need(pe, a_mix_sb, c(2))
                        t.transpose(bank_c[0:3 * GE, 0:128], gate_parts[:, :, :].rearrange("p s n -> p (s n)"),
                                    ident[:, :]).then_inc(g_T, 1)
                    if e == 1 and s.has(0):
                        if s.is_step(0):
                            pe.wait_ge(w_split, 5)
                        need(pe, g_T_sb, c(1))
                        need(pe, g_logits, c(1))
                        t.matmul(bank_a[:, :], gateT[:, :], b2_parts[:, :, :].rearrange("p g d -> p (g d)"),
                                 start=True, stop=True).then_inc(b_term, 1)
                    if e == 3 and s.has(2):
                        need(pe, a_prob, c(3))
                        need(pe, a_masked, c(3))
                        transposes(bank_b, [prob[:, j, :] for j in range(G)]).then_inc(a_probT, 1)
                    if e == 4 and s.has(2):
                        need(pe, a_probT_sb, c(3))
                        need(pe, a_norm, c(3))
                        need(pe, g_T_sb, c(1))
                        for j in range(G):
                            ins = t.matmul(bank_c[:, j * N:(j + 1) * N], x_norm[s.parity(2)][:, j, :], probT[:, j, :],
                                           start=True, stop=True)
                        ins.then_inc(a_mix, 1)
                    if e == 4 and s.has(1):
                        need(pe, f_norm, c(2))
                        need(pe, b_added, c(1))
                        need(pe, g_logits, c(1))
                        transposes(bank_a, [y_norm[:, j, :] for j in range(G)]).then_inc(f_yT, 1)
                    if e == 5 and s.has(2):
                        need(pe, a_mix_sb, c(3))
                        for j in range(G):
                            ins = t.matmul(bank_b[:, j * D:(j + 1) * D], mixT[:, j, :], W_sb[:, :],
                                           start=True, stop=True)
                        ins.then_inc(r_h, 1)
                    if e == 5 and s.has(1):
                        need(pe, f_xn, c(2))
                        need(pe, f_hi, c(2))
                        for j in range(G):
                            ins = t.matmul(bank_a[:, j * E:(j + 1) * E], xn[:, j * N:(j + 1) * N], Wr_sb[:, :],
                                           start=True, stop=True)
                        ins.then_inc(f_logits, 1)
                    if e == 4 and s.is_step(-2):
                        pe.wait_ge(ffn_loaded, 16 * 5)
                        t.transpose(bank_a[:, 0:uses], b1_rows[:, :], ident[0:uses, 0:uses]).then_inc(setup_pe, 1)
                        pe.wait_ge(setup_act, 3)

            run(pe, step)


_INS = ["x", "adj", "L0_gnn_W", "L0_gnn_a", "L0_gnn_gamma", "L0_gnn_beta", "L0_ffn_gamma", "L0_ffn_beta",
        "L0_ffn_Wr", "L0_ffn_br", "L0_ffn_W1", "L0_ffn_b1", "L0_ffn_W2", "L0_ffn_b2"]


def kernel(**inputs):
    import numpy as np
    import concourse.bacc as bacc
    from concourse.bass_utils import run_bass_kernel_spmd

    nc = bacc.Bacc("TRN2", target_bir_lowering=False, num_devices=1)
    arrays, args = {}, []
    for name in _INS:
        arr = np.ascontiguousarray(inputs[name])
        arrays[name + "_dram"] = arr
        args.append(nc.dram_tensor(name + "_dram", arr.shape, mybir.dt.from_np(arr.dtype), kind="ExternalInput").ap())
    shape = inputs["x"].shape
    args.append(nc.dram_tensor("out_dram", shape, F32, kind="ExternalOutput").ap())
    gat_moe_kernel(nc, *args)
    r = run_bass_kernel_spmd(nc, [arrays], core_ids=[0])
    return r.results[0]["out_dram"]
```
